# Optimizing a Trainium2 kernel written in Bass

```python
import numpy as np
import jax
import jax.numpy as jnp

def _softmax(x, axis=-1):
    return jax.nn.softmax(x, axis=axis)

def _gelu(x):
    return jax.nn.gelu(x, approximate=True)

def _silu(x):
    return jax.nn.silu(x)

def _sigmoid(x):
    return jax.nn.sigmoid(x)

def _layernorm(x, axis=-1, eps=1e-05):
    m = jnp.mean(x, axis=axis, keepdims=True)
    v = jnp.var(x, axis=axis, keepdims=True)
    return (x - m) / jnp.sqrt(v + eps)

def _scatter_add(tgt, idx, src, axis=0):
    return tgt.at[idx].add(src)

def _segment_sum(src, seg, n):
    return jax.ops.segment_sum(src, seg, n)
kernel_name = 'mk_gnn_resnorm_d1_gnn_r8_366a8a'

def setup_inputs(seed: int=0):
    np.random.seed(seed)
    _w = jnp.asarray

    def _rec_inputs():
        import jax
        import jax.numpy as jnp
        _gk = jax.random.key(seed)
        x = -0.0003713 + 1 * jax.random.normal(jax.random.fold_in(_gk, 1), (6250, 256), jnp.float32)
        src = jax.random.randint(jax.random.fold_in(_gk, 2), (200000,), 0, 6250, jnp.int32)
        dst = jnp.minimum((6250 * jax.random.uniform(jax.random.fold_in(_gk, 3), (200000,)) ** 2.0).astype(jnp.int32), 49999)
        _o = jnp.argsort(dst, stable=True)
        src = src[_o]
        dst = dst[_o]
        edge_attr_16 = -0.000153872 + 1.00011 * jax.random.normal(jax.random.fold_in(_gk, 11), (200000, 16), jnp.float32)
        edge_attr_4 = 0.0007022 + 0.999661 * jax.random.normal(jax.random.fold_in(_gk, 12), (200000, 4), jnp.float32)
        return (x, src, dst, edge_attr_16, edge_attr_4)
    x, src, dst, edge_attr_16, edge_attr_4 = _rec_inputs()

    def _L0_gnn_setup():
        import jax, jax.numpy as jnp
        import numpy as np
        N, E, C, R, HID = (6250, 62500, 64, 16, 64)
        key = jax.random.key(seed)
        ks = jax.random.split(key, 24)
        g = lambda k, shape, s=1.0: jax.random.normal(k, shape, dtype=jnp.float32) * s
        cs = C ** (-0.5)
        inp = {'h': g(ks[0], (N, 4 * C)), 'edge_index': jax.random.randint(ks[1], (2, E), 0, N), 'edge_sh': g(ks[2], (E, 4)), 'edge_rbf': g(ks[3], (E, R)), 'W_up0': g(ks[4], (C, C), cs), 'W_up1': g(ks[5], (C, C), cs), 'M1': g(ks[6], (R, HID), R ** (-0.5)), 'M2': g(ks[7], (HID, HID), HID ** (-0.5)), 'M3': g(ks[8], (HID, HID), HID ** (-0.5)), 'M4': g(ks[9], (HID, 4 * C), HID ** (-0.5)), 'W_lin0': g(ks[10], (C, C), cs), 'W_lin1': g(ks[11], (C, C), cs), 'Wsc0': g(ks[12], (C, C), cs), 'Wsc1': g(ks[13], (C, C), cs), 'Wc0': g(ks[14], (C, 5)), 'Wc1': g(ks[15], (C, 4)), 'WB0': g(ks[16], (C, C), cs), 'WB1': g(ks[17], (C, C), cs), 'gamma0': jnp.ones((C,), jnp.float32), 'beta0': jnp.zeros((C,), jnp.float32), 'gamma1': jnp.ones((C,), jnp.float32)}
        return inp
    _L0_gnn_all = _L0_gnn_setup()
    _L0_gnn_in = {k: v for k, v in _L0_gnn_all.items() if k in ('W_up0', 'W_up1', 'M1', 'M2', 'M3', 'M4', 'W_lin0', 'W_lin1', 'Wsc0', 'Wsc1', 'Wc0', 'Wc1', 'WB0', 'WB1', 'gamma0', 'beta0', 'gamma1')}
    del _L0_gnn_all
    return {'x': x, 'src': src, 'dst': dst, 'edge_attr_16': edge_attr_16, 'edge_attr_4': edge_attr_4, 'L0_gnn_W_up0': _L0_gnn_in['W_up0'], 'L0_gnn_W_up1': _L0_gnn_in['W_up1'], 'L0_gnn_M1': _L0_gnn_in['M1'], 'L0_gnn_M2': _L0_gnn_in['M2'], 'L0_gnn_M3': _L0_gnn_in['M3'], 'L0_gnn_M4': _L0_gnn_in['M4'], 'L0_gnn_W_lin0': _L0_gnn_in['W_lin0'], 'L0_gnn_W_lin1': _L0_gnn_in['W_lin1'], 'L0_gnn_Wsc0': _L0_gnn_in['Wsc0'], 'L0_gnn_Wsc1': _L0_gnn_in['Wsc1'], 'L0_gnn_Wc0': _L0_gnn_in['Wc0'], 'L0_gnn_Wc1': _L0_gnn_in['Wc1'], 'L0_gnn_WB0': _L0_gnn_in['WB0'], 'L0_gnn_WB1': _L0_gnn_in['WB1'], 'L0_gnn_gamma0': _L0_gnn_in['gamma0'], 'L0_gnn_beta0': _L0_gnn_in['beta0'], 'L0_gnn_gamma1': _L0_gnn_in['gamma1']}

def reference(x, src, dst, edge_attr_16, edge_attr_4, L0_gnn_W_up0, L0_gnn_W_up1, L0_gnn_M1, L0_gnn_M2, L0_gnn_M3, L0_gnn_M4, L0_gnn_W_lin0, L0_gnn_W_lin1, L0_gnn_Wsc0, L0_gnn_Wsc1, L0_gnn_Wc0, L0_gnn_Wc1, L0_gnn_WB0, L0_gnn_WB1, L0_gnn_gamma0, L0_gnn_beta0, L0_gnn_gamma1):
    import jax
    import jax.numpy as jnp

    def _L0_gnn_ref(h, edge_index, edge_sh, edge_rbf, W_up0, W_up1, M1, M2, M3, M4, W_lin0, W_lin1, Wsc0, Wsc1, Wc0, Wc1, WB0, WB1, gamma0, beta0, gamma1):
        import jax, jax.numpy as jnp
        import numpy as np
        N, E, C, R, HID = (6250, 62500, 64, 16, 64)
        n = h.shape[0]
        h0 = h[:, :C]
        h1 = h[:, C:].reshape(n, C, 3)
        up0 = h0 @ W_up0
        up1 = jnp.einsum('ncx,cd->ndx', h1, W_up1)
        r = jax.nn.silu(edge_rbf @ M1)
        r = jax.nn.silu(r @ M2)
        r = jax.nn.silu(r @ M3)
        tpw = (r @ M4).reshape(-1, 4, C)
        snd, rcv = (edge_index[0], edge_index[1])
        x0 = up0[snd]
        x1 = up1[snd]
        sh0 = edge_sh[:, 0]
        sh1 = edge_sh[:, 1:]
        inv3 = 1.0 / jnp.sqrt(jnp.float32(3.0))
        m0e = tpw[:, 0] * x0 * sh0[:, None] + tpw[:, 3] * jnp.einsum('ecx,ex->ec', x1, sh1) * inv3
        m1e = tpw[:, 1][:, :, None] * x0[:, :, None] * sh1[:, None, :] + tpw[:, 2][:, :, None] * x1 * sh0[:, None, None]
        msg0 = jax.ops.segment_sum(m0e, rcv, num_segments=n)
        msg1 = jax.ops.segment_sum(m1e, rcv, num_segments=n)
        A0 = msg0 @ W_lin0
        A1 = jnp.einsum('ncx,cd->ndx', msg1, W_lin1)
        sc0 = h0 @ Wsc0
        sc1 = jnp.einsum('ncx,cd->ndx', h1, Wsc1)
        vv = jnp.sum(A1 * A1, -1)
        B0 = Wc0[:, 0] * A0 + Wc0[:, 1] * A0 * A0 + Wc0[:, 2] * vv + Wc0[:, 3] * A0 ** 3 + Wc0[:, 4] * A0 * vv
        B1 = (Wc1[:, 0] + Wc1[:, 1] * A0 + Wc1[:, 2] * A0 * A0 + Wc1[:, 3] * vv)[..., None] * A1
        o0 = B0 @ WB0 + sc0
        o1 = jnp.einsum('ncx,cd->ndx', B1, WB1) + sc1
        eps = jnp.float32(1e-05)
        mu = jnp.mean(o0, 0)
        xc = o0 - mu
        var = jnp.mean(xc * xc, 0)
        n0 = xc * jax.lax.rsqrt(var + eps) * gamma0 + beta0
        nrm1 = jnp.mean(jnp.sum(o1 * o1, -1) / 3.0, 0)
        n1 = o1 * (jax.lax.rsqrt(nrm1 + eps) * gamma1)[None, :, None]
        return jnp.concatenate([n0, n1.reshape(n, 3 * C)], -1)
    edge_index = jnp.stack([src, dst])
    x = _layernorm(x + _L0_gnn_ref(x, edge_index, edge_attr_4, edge_attr_16, L0_gnn_W_up0, L0_gnn_W_up1, L0_gnn_M1, L0_gnn_M2, L0_gnn_M3, L0_gnn_M4, L0_gnn_W_lin0, L0_gnn_W_lin1, L0_gnn_Wsc0, L0_gnn_Wsc1, L0_gnn_Wc0, L0_gnn_Wc1, L0_gnn_WB0, L0_gnn_WB1, L0_gnn_gamma0, L0_gnn_beta0, L0_gnn_gamma1), axis=-1)
    return x

_drawn_inputs = setup_inputs


def setup_inputs(seed=0):
    import zlib

    import numpy as np

    out = dict(_drawn_inputs(seed))
    spreads = {'L0_gnn_gamma0': (1.0, 0.2), 'L0_gnn_beta0': (0.0, 0.1), 'L0_gnn_gamma1': (1.0, 0.2)}
    factors = {'L0_gnn_Wsc0': 8.0, 'L0_gnn_Wsc1': 8.0}
    for name, (base, spread) in spreads.items():
        noise = np.random.default_rng([zlib.crc32(name.encode()), seed]).standard_normal(out[name].shape)
        drawn = base * np.exp(spread * noise) if base else spread * noise
        out[name] = jnp.asarray(drawn.astype(out[name].dtype))
    for name, factor in factors.items():
        out[name] = (out[name] * factor).astype(out[name].dtype)
    return out
```

```python
from contextlib import ExitStack

import concourse.bass as bass
from concourse import mybir
from concourse.alu_op_type import AluOpType as ALU

ACT = mybir.ActivationFunctionType
AX = mybir.AxisListType
F32 = mybir.dt.float32
I32 = mybir.dt.int32

P = 128
C = 64
J = 4
F = J * C
TG = 8
GE = TG * P
SLOTS = 4
WINDOW = P
EPS = 1e-5


class Shapes:

    def __init__(self, nodes, edges):
        self.nodes = nodes
        self.edges = edges
        self.pairs = 2 * (-(-nodes // (4 * P)))
        self.half = self.pairs * P
        self.rows = 2 * self.half
        self.second = nodes - self.half
        self.groups = SLOTS * (-(-edges // (GE * SLOTS)))
        self.tiles = self.groups * TG
        self.padded_edges = self.groups * GE
        self.dump = self.rows
        self.sum_rows = self.rows + P


def at_least(engine, semaphore, value):
    if isinstance(value, int) and value <= 0:
        return
    engine.wait_ge(semaphore, value)


def clear(engine, passed):
    engine.sem_inc(passed, 1)


def run_steps(engine, step, steps, extra):
    first = 2 * SLOTS
    last = steps - SLOTS
    for g in range(min(first, steps)):
        step(g // SLOTS, g % SLOTS)
    if last > first:
        with engine.Fori(first // SLOTS, last // SLOTS) as i:
            for u in range(SLOTS):
                step(i, u)
    for g in range(max(last, first), steps + extra):
        step(g // SLOTS, g % SLOTS)


def in_pairs(engine, step, count):
    bodies = count // 2
    for n in range(min(4, count)):
        step(n // 2, n % 2)
    if bodies > 3:
        with engine.Fori(2, bodies - 1) as i:
            for s in range(2):
                step(i, s)
    for n in range(max(4, count - 2), count):
        step(n // 2, n % 2)


def slot_of(i, u, ahead=0):
    return i + (u + ahead) // SLOTS, (u + ahead) % SLOTS


def build(nc, x_cm, src_idx, dst_pt, dst_rows, first_dst, sh_in, rbf_in, weights, out, sizes):
    sz = sizes
    G = sz.groups
    with ExitStack() as top:
        def sem(name):
            return top.enter_context(nc.semaphore(name))

        def keep(name, shape, dt=F32):
            return top.enter_context(nc.sbuf_tensor(name, shape, dt))

        up_dram = nc.dram_tensor("up_rows", (sz.rows, F), F32, kind="Internal").ap()
        sums_dram = nc.dram_tensor("message_sums", (sz.sum_rows, F), F32, kind="Internal").ap()

        identity = keep("identity", [P, P])
        fold_halves = keep("fold_halves", [P, P])
        w_up = keep("w_up", [P, 2, P])
        w_lin = keep("w_lin", [P, 2, P])
        w_self = keep("w_self", [P, 2, P])
        w_back = keep("w_back", [P, 2, P])
        w_m1 = keep("w_m1", [32, P])
        w_m2 = keep("w_m2", [P, P])
        w_m3 = keep("w_m3", [P, P])
        w_m4 = keep("w_m4", [P, 2 * F])
        poly0 = keep("poly0", [P, 5])
        poly1 = keep("poly1", [P, 4])
        affine = keep("affine", [P, 3])
        eps_col = keep("eps_col", [P, 1])
        lane_row = keep("lane_row", [P, P])
        lane_col = keep("lane_col", [P, 1])
        rel = keep("rel", [P, sz.tiles])
        dst_f = keep("dst_f", [P, sz.tiles])
        window_rows = keep("window_rows", [P, G], I32)
        lower = keep("lower", [P, P])
        misfit = keep("misfit", [1, 1], I32)

        with ExitStack() as ctx:
            def sb(name, shape, dt=F32):
                return ctx.enter_context(nc.sbuf_tensor(name, shape, dt))

            zeros = sb("zeros", [P, F])
            lane_row_i = sb("lane_row_i", [P, P], I32)
            lane_col_i = sb("lane_col_i", [P, 1], I32)
            ones = sb("ones", [P, P])
            dst_i = sb("dst_i", [P, sz.tiles], I32)
            base_i = sb("base_i", [P, G], I32)
            base_f = sb("base_f", [P, G])
            rows_f = sb("rows_f", [P, G])
            far = sb("far", [P, 4])
            CH = 2
            x_ring = [sb(f"x_ring{s}", [P, J, CH * P]) for s in range(2)]
            up_sb = [sb(f"up_sb{s}", [P, CH, 2, J, C]) for s in range(2)]
            up_ps = [[ctx.enter_context(nc.psum_tensor(f"up_ps{s}_{q}", [P, J, 2, C], F32))
                      for q in range(CH)] for s in range(2)]
            count_ps = ctx.enter_context(nc.psum_tensor("count_ps", [P, 1], F32))

            blank = sem("p1_blank")
            weights_in = sem("p1_weights_in")
            dst_in = sem("p1_dst_in")
            x_in = [sem(f"p1_x_in{s}") for s in range(2)]
            up_done = sem("p1_up_done")
            act_copied = sem("p1_act_copied")
            dve_copied = sem("p1_dve_copied")
            up_out = [sem(f"p1_up_out{s}") for s in range(2)]
            zero_made = sem("p1_zero_made")
            zeroed = sem("p1_zeroed")
            patterns = sem("p1_patterns")
            dve_step = sem("p1_dve_step")
            far_made = sem("p1_far_made")
            counted = sem("p1_counted")

            chunks = sz.pairs // CH

            def by_chunk(engine, step):
                in_pairs(engine, step, chunks // 2 * 2)
                if chunks % 2:
                    step(chunks // 2, 0)

            W = weights
            blocks = [(w_up, "W_up"), (w_lin, "W_lin"), (w_self, "Wsc"), (w_back, "WB")]
            block = ctx.enter_context(nc.Block())

            @block.sync
            def _(sp):
                sp.dma_start(dst_i[:, :], dst_pt).then_inc(dst_in, 16)
                sp.dma_start(base_i[:, :], first_dst.to_broadcast([P, G])).then_inc(dst_in, 16)

                def load(i, s):
                    k = 2 * i + s
                    at_least(sp, up_done, CH * (k - 1))
                    sp.dma_start(x_ring[s][:, :, :],
                                 x_cm[:, :, bass.ds(k * (CH * P), CH * P)]).then_inc(x_in[s], 16)

                by_chunk(sp, load)
                sp.wait_ge(zero_made, 1)
                for r in range(sz.sum_rows // P):
                    sp.dma_start(sums_dram[r * P:(r + 1) * P, :], zeros[:, :]).then_inc(zeroed, 16)
                sp.wait_ge(zeroed, 16 * (sz.sum_rows // P))
                for s in range(2):
                    sp.wait_ge(up_out[s], 32 * ((chunks + 1 - s) // 2))

            @block.gpsimd
            def _(pool):
                nc.gpsimd.memset(identity[:, :], 0.0).then_inc(patterns, 1)
                nc.gpsimd.memset(lower[:, :], 1.0).then_inc(patterns, 1)
                nc.gpsimd.iota(lane_row_i[:, :], [[1, P]], base=0, channel_multiplier=0).then_inc(patterns, 1)
                nc.gpsimd.iota(lane_col_i[:, :], [[0, 1]], base=0, channel_multiplier=1).then_inc(patterns, 1)
                pool.wait_ge(patterns, 4)
                nc.gpsimd.affine_select(out=identity[:, :], in_=identity[:, :], compare_op=ALU.not_equal,
                                        fill=1.0, base=0, pattern=[[-1, P]],
                                        channel_multiplier=1).then_inc(patterns, 1)
                nc.gpsimd.affine_select(out=lower[:, :], in_=lower[:, :], compare_op=ALU.is_gt,
                                        fill=0.0, base=0, pattern=[[-1, P]],
                                        channel_multiplier=1).then_inc(patterns, 1)

            @block.scalar
            def _(act):
                act.wait_ge(blank, 1)
                for w, name in blocks:
                    for v in range(2):
                        for h in range(2):
                            act.dma_start(w[h * C:(h + 1) * C, v, h * C:(h + 1) * C],
                                          W[f"{name}{v}"]).then_inc(weights_in, 16)
                for h in range(2):
                    rows = slice(h * C, (h + 1) * C)
                    act.dma_start(w_m1[h * 16:(h + 1) * 16, rows], W["M1"]).then_inc(weights_in, 16)
                    act.dma_start(w_m2[rows, rows], W["M2"]).then_inc(weights_in, 16)
                    act.dma_start(w_m3[rows, rows], W["M3"]).then_inc(weights_in, 16)
                    for place, part in enumerate((0, 2, 3, 1)):
                        at = h * F + place * C
                        act.dma_start(w_m4[rows, at:at + C],
                                      W["M4"][:, part * C:(part + 1) * C]).then_inc(weights_in, 16)
                    act.dma_start(poly0[rows, :], W["Wc0"]).then_inc(weights_in, 16)
                    act.dma_start(poly1[rows, :], W["Wc1"]).then_inc(weights_in, 16)
                    for n, name in enumerate(("gamma0", "beta0", "gamma1")):
                        act.dma_start(affine[rows, n:n + 1],
                                      W[name].rearrange("(c o) -> c o", o=1)).then_inc(weights_in, 16)

                def project(i, s):
                    k = 2 * i + s
                    at_least(act, up_out[s], 32 * i)
                    act.wait_ge(up_done, CH * k + 1)
                    nc.scalar.activation(up_sb[s][:, 0, :, :, :].rearrange("p h j c -> p j h c"),
                                         up_ps[s][0][:, :, :, :], ACT.Copy).then_inc(act_copied, 1)
                    act.wait_ge(act_copied, k + 1)
                    act.wait_ge(dve_copied, k + 1)
                    for h in range(2):
                        act.dma_start(
                            up_dram[bass.ds(k * (CH * P) + h * sz.half, CH * P), :]
                            .rearrange("(q p) f -> p q f", p=P),
                            up_sb[s][:, :, h, :, :].rearrange("p q j c -> p q (j c)"),
                        ).then_inc(up_out[s], 16)

                by_chunk(act, project)

            @block.vector
            def _(dve):
                for w, _name in blocks:
                    nc.vector.memset(w[:, :, :], 0.0)
                nc.vector.memset(w_m1[:, :], 0.0)
                nc.vector.memset(w_m2[:, :], 0.0)
                nc.vector.memset(w_m3[:, :], 0.0)
                nc.vector.memset(w_m4[:, :], 0.0).then_inc(blank, 1)
                nc.vector.memset(zeros[:, :], 0.0).then_inc(zero_made, 1)
                nc.vector.memset(ones[:, :], 1.0)
                nc.vector.memset(eps_col[:, :], EPS).then_inc(dve_step, 1)

                def project(i, s):
                    k = 2 * i + s
                    at_least(dve, up_out[s], 32 * i)
                    dve.wait_ge(up_done, CH * k + 2)
                    nc.vector.tensor_copy(up_sb[s][:, 1, :, :, :].rearrange("p h j c -> p j h c"),
                                          up_ps[s][1][:, :, :, :]).then_inc(dve_copied, 1)

                by_chunk(dve, project)
                dve.wait_ge(patterns, 6)
                nc.vector.tensor_copy(lane_row[:, :], lane_row_i[:, :])
                nc.vector.tensor_copy(lane_col[:, :], lane_col_i[:, :])
                for h in range(2):
                    cols = slice(h * C, (h + 1) * C)
                    nc.vector.tensor_tensor(fold_halves[:, cols], identity[:, 0:C], identity[:, C:P], ALU.add)
                dve.wait_ge(dst_in, 32)
                nc.vector.tensor_copy(dst_f[:, :], dst_i[:, :])
                nc.vector.tensor_copy(base_f[:, :], base_i[:, :]).then_inc(dve_step, 1)
                dve.wait_ge(dve_step, 2)
                nc.vector.tensor_tensor(rel[:, :].rearrange("p (g t) -> p g t", t=TG),
                                        dst_f[:, :].rearrange("p (g t) -> p g t", t=TG),
                                        base_f[:, :].unsqueeze(2).to_broadcast([P, G, TG]), ALU.subtract)
                nc.vector.tensor_scalar(rows_f[:, :], base_f[:, :], lane_col[:, 0:1], None,
                                        ALU.add).then_inc(dve_step, 1)
                dve.wait_ge(dve_step, 3)
                nc.vector.tensor_copy(window_rows[:, :], rows_f[:, :])
                nc.vector.tensor_reduce(far[:, 0:1], rel[:, :], AX.X, ALU.max)
                nc.vector.tensor_reduce(far[:, 1:2], rel[:, :], AX.X, ALU.min).then_inc(dve_step, 1)
                dve.wait_ge(dve_step, 4)
                nc.vector.tensor_scalar(far[:, 2:3], far[:, 0:1], float(WINDOW), None, ALU.is_ge)
                nc.vector.tensor_scalar(far[:, 3:4], far[:, 1:2], 0.0, None, ALU.is_lt).then_inc(dve_step, 1)
                dve.wait_ge(dve_step, 5)
                nc.vector.tensor_tensor(far[:, 0:1], far[:, 2:3], far[:, 3:4], ALU.add).then_inc(far_made, 1)
                dve.wait_ge(counted, 1)
                nc.vector.tensor_copy(misfit[:, :], count_ps[0:1, :]).then_inc(dve_step, 1)
                dve.wait_ge(weights_in, 16 * (16 + 2 * (3 + 4 + 2 + 3)))
                for h in range(2):
                    dots = w_m4[:, h * F + 2 * C:h * F + 3 * C]
                    nc.vector.tensor_scalar(dots, dots, float(3.0 ** -0.5), None, ALU.mult).then_inc(dve_step, 1)
                dve.wait_ge(dve_step, 8)

            @block.tensor
            def _(pe):
                pe.wait_ge(weights_in, 16 * (16 + 2 * (3 + 4 + 2 + 3)))

                def project(i, s):
                    k = 2 * i + s
                    pe.wait_ge(x_in[s], 16 * (i + 1))
                    at_least(pe, act_copied, k - 1)
                    at_least(pe, dve_copied, k - 1)
                    for q in range(CH):
                        for j in range(J):
                            last = nc.tensor.matmul(up_ps[s][q][:, j, :, :],
                                                    x_ring[s][:, j, q * P:(q + 1) * P],
                                                    w_up[:, min(j, 1), :], start=True, stop=True)
                        last.then_inc(up_done, 1)

                by_chunk(pe, project)
                pe.wait_ge(far_made, 1)
                nc.tensor.matmul(count_ps[:, :], ones[:, :], far[:, 0:1], start=True, stop=True).then_inc(counted, 1)

        for general in (False, True):
            edges(nc, sz, general, up_dram, sums_dram, src_idx, dst_rows, sh_in, rbf_in,
                  w_m1, w_m2, w_m3, w_m4, lane_row, lane_col, lower, rel, dst_f, window_rows, misfit)

        node_phase(nc, sz, x_cm, sums_dram, out, identity, fold_halves, w_lin, w_self, w_back,
                   poly0, poly1, affine, eps_col)


def edges(nc, sz, general, up_dram, sums_dram, src_idx, dst_rows, sh_in, rbf_in,
          w_m1, w_m2, w_m3, w_m4, lane_row, lane_col, lower, rel, dst_f, window_rows, misfit):
    G = sz.groups
    tag = "any_" if general else "win_"
    reduce_lag = 2
    copy_lag = 2 if general else 3
    scatter_lag = 5 if general else 6
    per_group = TG if general else 1
    with ExitStack() as ctx:
        def sb(name, shape, dt=F32):
            return ctx.enter_context(nc.sbuf_tensor(tag + name, shape, dt))

        def ps(name, shape):
            return ctx.enter_context(nc.psum_tensor(tag + name, shape, F32))

        def sem(name):
            return ctx.enter_context(nc.semaphore(tag + name))

        idx = [sb(f"idx{s}", [P, TG], I32) for s in range(SLOTS)]
        sh = [sb(f"sh{s}", [P, TG, 4]) for s in range(SLOTS)]
        rbf = [sb(f"rbf{s}", [32, 4 * P]) for s in range(SLOTS)]
        X = [sb(f"X{s}", [P, TG, C + F]) for s in range(SLOTS)]
        hid1 = sb("hid1", [P, 4 * P])
        hid2 = sb("hid2", [P, 4 * P])
        hid3 = [sb(f"hid3_{s}", [P, 4 * P]) for s in range(2)]
        scaled = [sb(f"scaled{s}", [P, TG, 2, C]) for s in range(2)]
        dots = [sb(f"dots{s}", [P, TG, 3, C]) for s in range(2)]
        dot01 = sb("dot01", [P, TG, C])
        part = sb("part", [P, TG, 5, C])
        msg = [sb(f"msg{s}", [P, TG, J, C]) for s in range(2)]
        hot = [sb(f"hot{s}", [P, TG, P]) for s in range(2)]
        sums = [sb(f"sums{s}", [P, F]) for s in range(2)]
        sums_at = [sb(f"sums_at{s}", [P, 1], I32) for s in range(2)]
        if general:
            drow_i = [sb(f"drow_i{s}", [P, TG * P], I32) for s in range(SLOTS)]
            drow_f = sb("drow_f", [P, TG, P])
            before = sb("before", [P, TG, P])
            earlier = sb("earlier", [P, TG])
            spare = sb("spare", [P, TG])
            rows_i = [sb(f"rows_i{s}", [P, TG], I32) for s in range(2)]
        hid_ps = [ps(f"hid_ps{b}", [P, 4 * P]) for b in range(2)]
        tpw_ps = [ps(f"tpw_ps{b}", [P, 2, J, C]) for b in range(4)]
        sum_ps = [ps(f"sum_ps{b}", [P, F]) for b in range(2)]

        loaded = [sem(f"loaded{s}") for s in range(SLOTS)]
        gathered = [sem(f"gathered{s}") for s in range(SLOTS)]
        mm1, mm2, mm3 = sem("mm1"), sem("mm2"), sem("mm3")
        act1, act2, act3 = sem("act1"), sem("act2"), sem("act3")
        mm4 = sem("mm4")
        scaled_done = sem("scaled_done")
        dots_done = sem("dots_done")
        dot01_done, u_done = sem("dot01_done"), sem("u_done")
        part_done = sem("part_done")
        hot_done = sem("hot_done")
        cross_done = sem("cross_done")
        own_done = sem("own_done")
        msg_done = sem("msg_done")
        summed = sem("summed")
        sums_out = sem("sums_out")
        scattered = sem("scattered")
        gathers_cleared, scatters_cleared = sem("gathers_cleared"), sem("scatters_cleared")
        rank_step = sem("rank_step")

        enter = ctx.enter_context(nc.Block())
        block = enter
        n_in = 4 if general else 3

        def chosen(engine):
            count = engine.value_load(misfit[0:1, 0:1], min_val=0, max_val=P)
            return engine.If(count > 0 if general else count < 1)

        @block.sync
        def _(sp):
            def step(i, u):
                g = SLOTS * i + u
                if isinstance(g, int) and g >= G:
                    return
                at_least(sp, msg_done, g - SLOTS + 1)
                sp.dma_start(rbf[u][:, :], rbf_in[bass.ds(g * 32, 32), :]).then_inc(loaded[u], 16)
                sp.dma_start(idx[u][:, :], src_idx[bass.ds(g * P, P), :]).then_inc(loaded[u], 16)
                sp.dma_start(sh[u][:, :, :].rearrange("p t k -> p (t k)"),
                             sh_in[bass.ds(g * P, P), :]).then_inc(loaded[u], 16)
                if general:
                    sp.dma_start(drow_i[u][:, :],
                                 dst_rows[bass.ds(g, 1), :].to_broadcast([P, GE])).then_inc(loaded[u], 16)

            with chosen(sp):
                run_steps(sp, step, G, 0)
                sp.wait_ge(scattered, 16 * G * per_group)

        @block.gpsimd
        def _(pool):
            def step(i, u):
                g = SLOTS * i + u
                static = isinstance(g, int)
                if not (static and g >= G):
                    pool.wait_ge(loaded[u], 16 * n_in * (i + 1))
                    at_least(pool, msg_done, g - SLOTS + 1)
                    clear(pool, gathers_cleared)
                    for t in range(TG):
                        pool.indirect_dma_start(
                            out=X[u][:, t, C:C + F], out_offset=None, in_=up_dram[:, :],
                            in_offset=bass.IndirectOffsetOnAxis(ap=idx[u][:, t:t + 1], axis=0),
                        ).then_inc(gathered[u], 16)
                done = g - scatter_lag
                if static and not 0 <= done < G:
                    return
                su = (u - scatter_lag) % 2
                for t in range(per_group):
                    n = done * per_group + t
                    s = t % 2 if general else su
                    pool.wait_ge(sums_out, 2 * (n + 1))
                    at_least(pool, scattered, 16 * n)
                    clear(pool, scatters_cleared)
                    pool.indirect_dma_start(
                        out=sums_dram[:, :],
                        out_offset=bass.IndirectOffsetOnAxis(ap=sums_at[s][:, 0:1], axis=0),
                        in_=sums[s][:, :], in_offset=None, compute_op=ALU.add,
                    ).then_inc(scattered, 16)

            with chosen(pool):
                run_steps(pool, step, G, scatter_lag)

        @block.tensor
        def _(pe):
            def layer1(i, u):
                g = SLOTS * i + u
                pe.wait_ge(loaded[u], 16 * n_in * (i + 1))
                at_least(pe, act2, g)
                nc.tensor.matmul(hid_ps[u % 2][:, :], w_m1[:, :], rbf[u][:, :],
                                 start=True, stop=True).then_inc(mm1, 1)

            def layer2(i, u):
                pe.wait_ge(act1, SLOTS * i + u + 1)
                nc.tensor.matmul(hid_ps[(u + 1) % 2][:, :], w_m2[:, :], hid1[:, :],
                                 start=True, stop=True).then_inc(mm2, 1)

            def layer3(i, u):
                pe.wait_ge(act2, SLOTS * i + u + 1)
                nc.tensor.matmul(hid_ps[u % 2][:, :], w_m3[:, :], hid2[:, :],
                                 start=True, stop=True).then_inc(mm3, 1)

            def layer4(g, u, q):
                if q == 0:
                    pe.wait_ge(act3, g + 1)
                at_least(pe, part_done, 4 * g - 4 + q + 1)
                nc.tensor.matmul(tpw_ps[q][:, :, :, :], hid3[u % 2][:, q * P:(q + 1) * P],
                                 w_m4[:, :], start=True, stop=True).then_inc(mm4, 1)

            def reduce_group(g, u):
                pe.wait_ge(hot_done, g + 1)
                pe.wait_ge(msg_done, g + 1)
                if not general:
                    at_least(pe, sums_out, 2 * (g - 1))
                for t in range(TG):
                    n = g * TG + t
                    if general:
                        at_least(pe, sums_out, 2 * (n - 1))
                    b = t % 2 if general else u % 2
                    done = nc.tensor.matmul(sum_ps[b][:, :], hot[u % 2][:, t, :],
                                            msg[u % 2][:, t, :, :],
                                            start=general or t == 0, stop=general or t == TG - 1)
                    if general:
                        done.then_inc(summed, 1)
                if not general:
                    done.then_inc(summed, 1)

            def step(i, u):
                g = SLOTS * i + u
                static = isinstance(g, int)
                ni, nu = slot_of(i, u, 1)
                ahead = not (static and g + 1 >= G)
                here = not (static and g >= G)
                if ahead:
                    layer1(ni, nu)
                if here:
                    layer4(g, u, 0)
                    layer4(g, u, 1)
                if ahead:
                    layer2(ni, nu)
                if here:
                    layer4(g, u, 2)
                    layer4(g, u, 3)
                if ahead:
                    layer3(ni, nu)
                if not (static and g < reduce_lag):
                    reduce_group(g - reduce_lag, (u - reduce_lag) % SLOTS)

            with chosen(pe):
                layer1(0, 0)
                layer2(0, 0)
                layer3(0, 0)
                run_steps(pe, step, G, reduce_lag)

        @block.scalar
        def _(act):
            def silu(layer, i, u):
                g = SLOTS * i + u
                ready = (mm1, mm2, mm3)[layer]
                out = (hid1, hid2, hid3[u % 2])[layer]
                bank = hid_ps[(u + layer % 2) % 2]
                act.wait_ge(ready, g + 1)
                nc.scalar.activation(out[:, :], bank[:, :], ACT.Silu).then_inc((act1, act2, act3)[layer], 1)

            def scale_weights(g, u, q):
                if q == 0:
                    at_least(act, own_done, 2 * (g - 1))
                act.wait_ge(mm4, 4 * g + q + 1)
                for h in range(2):
                    t = q + 4 * h
                    done = nc.scalar.activation(scaled[u % 2][:, t, :, :], tpw_ps[q][:, h, 0:2, :],
                                                ACT.Copy, scale=sh[u][:, t, 0:1])
                done.then_inc(scaled_done, 1)

            def dot_products(i, u, tiles):
                g = SLOTS * i + u
                if tiles[0] == 0:
                    act.wait_ge(loaded[u], 16 * n_in * (i + 1))
                    act.wait_ge(gathered[u], 16 * TG * (i + 1))
                    at_least(act, u_done, g - 1)
                for t in tiles:
                    for k in range(3):
                        done = nc.scalar.activation(dots[u % 2][:, t, k, :],
                                                    X[u][:, t, (2 + k) * C:(3 + k) * C],
                                                    ACT.Copy, scale=sh[u][:, t, k + 1:k + 2])
                if tiles[-1] == TG - 1:
                    done.then_inc(dots_done, 1)

            def copy_sums(g, u):
                for t in range(per_group):
                    n = g * per_group + t
                    b = t % 2 if general else u % 2
                    act.wait_ge(summed, n + 1)
                    at_least(act, scattered, 16 * (n - 1))
                    nc.scalar.activation(sums[b][:, :], sum_ps[b][:, :], ACT.Copy).then_inc(sums_out, 1)
                    if general:
                        at = rows_i[u % 2][:, t:t + 1]
                    else:
                        at = window_rows[:, bass.ds(g, 1)]
                    nc.scalar.copy(sums_at[b][:, :], at).then_inc(sums_out, 1)

            def step(i, u):
                g = SLOTS * i + u
                static = isinstance(g, int)
                ni, nu = slot_of(i, u, 1)
                ahead = not (static and g + 1 >= G)
                here = not (static and g >= G)
                if ahead:
                    silu(0, ni, nu)
                    dot_products(ni, nu, (0,))
                if here:
                    scale_weights(g, u, 0)
                    scale_weights(g, u, 1)
                if ahead:
                    dot_products(ni, nu, (1,))
                    silu(1, ni, nu)
                if here:
                    scale_weights(g, u, 2)
                if ahead:
                    dot_products(ni, nu, (2,))
                if here:
                    scale_weights(g, u, 3)
                if ahead:
                    silu(2, ni, nu)
                    dot_products(ni, nu, range(3, TG))
                if not (static and not 0 <= g - copy_lag < G):
                    copy_sums(g - copy_lag, (u - copy_lag) % SLOTS)

            with chosen(act):
                silu(0, 0, 0)
                silu(1, 0, 0)
                silu(2, 0, 0)
                dot_products(0, 0, range(TG))
                run_steps(act, step, G, copy_lag)

        @block.vector
        def _(dve):
            def make_hot(g, i, u):
                if general:
                    dve.wait_ge(loaded[u], 16 * n_in * (i + 1))
                at_least(dve, summed, per_group * (g - 1))
                here = (dst_f if general else rel)[:, bass.ds(g * TG, TG)].unsqueeze(2).to_broadcast([P, TG, P])
                if general:
                    nc.vector.tensor_copy(drow_f[:, :, :], drow_i[u][:, :].rearrange("p (t e) -> p t e", t=TG)) \
                        .then_inc(rank_step, 1)
                    dve.wait_ge(rank_step, 4 * g + 1)
                    lanes = drow_f[:, :, :]
                else:
                    lanes = lane_row[:, :].unsqueeze(1).to_broadcast([P, TG, P])
                nc.vector.tensor_tensor(hot[u % 2][:, :, :], lanes, here, ALU.is_equal).then_inc(hot_done, 1)

            def rank(g, u):
                at_least(dve, sums_out, 2 * TG * (g - 1))
                dve.wait_ge(hot_done, g + 1)
                nc.vector.tensor_tensor(before[:, :, :], hot[u % 2][:, :, :],
                                        lower[:, :].unsqueeze(1).to_broadcast([P, TG, P]),
                                        ALU.mult).then_inc(rank_step, 1)
                dve.wait_ge(rank_step, 4 * g + 2)
                nc.vector.tensor_reduce(earlier[:, :], before[:, :, :], AX.X, ALU.add)
                nc.vector.tensor_scalar(spare[:, :], dst_f[:, bass.ds(g * TG, TG)], -1.0,
                                        float(sz.dump), ALU.mult, ALU.add).then_inc(rank_step, 1)
                dve.wait_ge(rank_step, 4 * g + 3)
                nc.vector.tensor_scalar(earlier[:, :], earlier[:, :], 0.0, None, ALU.is_gt)
                nc.vector.tensor_scalar(spare[:, :], spare[:, :], lane_col[:, 0:1], None,
                                        ALU.add).then_inc(rank_step, 1)
                dve.wait_ge(rank_step, 4 * g + 4)
                nc.vector.tensor_tensor(spare[:, :], spare[:, :], earlier[:, :], ALU.mult).then_inc(cross_done, 1)
                dve.wait_ge(cross_done, 2 * g + 1)
                nc.vector.tensor_tensor(rows_i[u % 2][:, :], spare[:, :], dst_f[:, bass.ds(g * TG, TG)], ALU.add)

            def sum_first(g, u):
                dve.wait_ge(dots_done, g + 1)
                nc.vector.tensor_tensor(dot01[:, :, :], dots[u % 2][:, :, 0, :], dots[u % 2][:, :, 1, :],
                                        ALU.add).then_inc(dot01_done, 1)

            def sum_last(g, u):
                dve.wait_ge(dot01_done, g + 1)
                nc.vector.tensor_tensor(X[u][:, :, 0:C], dot01[:, :, :], dots[u % 2][:, :, 2, :],
                                        ALU.add).then_inc(u_done, 1)

            def step(i, u):
                g = SLOTS * i + u
                static = isinstance(g, int)
                if static and g >= G:
                    return
                ahead = not (static and g + 1 >= G)
                nu = (u + 1) % SLOTS
                crosses = 2 * g + 2 if general else g + 1
                x = X[u]
                dve.wait_ge(u_done, g + 1)
                at_least(dve, msg_done, g)
                for q in range(4):
                    dve.wait_ge(scaled_done, 4 * g + q + 1)
                    nc.vector.tensor_tensor(
                        part[:, q::4, 0::4, :], tpw_ps[q][:, :, 2:4, :],
                        x[:, q::4, 0:2 * C].rearrange("p t (b c) -> p t b c", b=2), ALU.mult,
                    ).then_inc(part_done, 1)
                if general:
                    make_hot(g, i, u)
                    rank(g, u)
                at_least(dve, summed, per_group * (g - 1))
                nc.vector.tensor_tensor(msg[u % 2][:, :, 0, :], scaled[u % 2][:, :, 0, :],
                                        x[:, :, C:2 * C], ALU.mult).then_inc(own_done, 1)
                nc.vector.tensor_tensor(msg[u % 2][:, :, 1:4, :],
                                        scaled[u % 2][:, :, 1:2, :].to_broadcast([P, TG, 3, C]),
                                        x[:, :, 2 * C:5 * C].rearrange("p t (k c) -> p t k c", k=3),
                                        ALU.mult).then_inc(own_done, 1)
                dve.wait_ge(part_done, 4 * g + 4)
                nc.vector.tensor_tensor(part[:, :, 1:4, :], part[:, :, 4:5, :].to_broadcast([P, TG, 3, C]),
                                        sh[u][:, :, 1:4].unsqueeze(3).to_broadcast([P, TG, 3, C]),
                                        ALU.mult).then_inc(cross_done, 1)
                if ahead:
                    sum_first(g + 1, nu)
                dve.wait_ge(cross_done, crosses)
                dve.wait_ge(own_done, 2 * g + 2)
                nc.vector.tensor_tensor(msg[u % 2][:, :, :, :], msg[u % 2][:, :, :, :],
                                        part[:, :, 0:4, :], ALU.add).then_inc(msg_done, 1)
                if ahead:
                    sum_last(g + 1, nu)
                if not general:
                    make_hot(g, i, u)

            with chosen(dve):
                sum_first(0, 0)
                sum_last(0, 0)
                run_steps(dve, step, G, 0)


def node_phase(nc, sz, x_cm, sums_dram, out, identity, fold_halves, w_lin, w_self, w_back,
               poly0, poly1, affine, eps_col):
    N = sz.pairs
    with ExitStack() as ctx:
        def sb(name, shape, dt=F32):
            return ctx.enter_context(nc.sbuf_tensor("node_" + name, shape, dt))

        def ps(name, shape):
            return ctx.enter_context(nc.psum_tensor("node_" + name, shape, F32))

        def sem(name):
            return ctx.enter_context(nc.semaphore("node_" + name))

        x = sb("x", [P, J, sz.half])
        o = sb("o", [P, J, sz.half])
        squares = sb("squares", [P, 3, sz.half])
        rows = [sb(f"rows{s}", [P, J, 2, C]) for s in range(2)]
        msg_t = [sb(f"msg_t{s}", [P, J, P]) for s in range(2)]
        a = [sb(f"a{s}", [P, J, P]) for s in range(2)]
        a_sq = [sb(f"a_sq{s}", [P, 3, P]) for s in range(2)]
        b = [sb(f"b{s}", [P, J, P]) for s in range(2)]
        vv = [sb(f"vv{s}", [P, P]) for s in range(2)]
        acc0 = sb("acc0", [P, P])
        acc1 = sb("acc1", [P, P])
        tr_ps = [ps(f"tr_ps{s}", [P, J, P]) for s in range(2)]
        a_ps = [ps(f"a_ps{s}", [P, J, P]) for s in range(2)]
        o_ps = [ps(f"o_ps{s}", [P, J, P]) for s in range(2)]
        stat_ps = ps("stat_ps", [P, 3])
        total = sb("total", [P, 3])
        mean = sb("mean", [P, 2])
        power = sb("power", [P, 2])
        root = sb("root", [P, 2])
        gain = sb("gain", [P, 4])
        shift = sb("shift", [P, 2])
        z = [sb(f"z{s}", [P, J, P]) for s in range(2)]
        bn = [sb(f"bn{s}", [P, 2, 6]) for s in range(2)]
        mv = [sb(f"mv{s}", [P, 2, 2]) for s in range(2)]
        sd = [sb(f"sd{s}", [P, 2]) for s in range(2)]
        rs = [sb(f"rs{s}", [P, 2]) for s in range(2)]
        nb = [sb(f"nb{s}", [P, 2]) for s in range(2)]
        y = [sb(f"y{s}", [P, 2, F]) for s in range(2)]

        x_in = sem("x_in")
        rows_in = [sem(f"rows_in{s}") for s in range(2)]
        turned, turned_out = sem("turned"), sem("turned_out")
        a_done, a_out = sem("a_done"), sem("a_out")
        vv_done, poly_step, b_done = sem("vv_done"), sem("poly_step"), sem("b_done")
        o_done, o_out = sem("o_done"), sem("o_out")
        total0, mean_done, totals12 = sem("total0"), sem("mean_done"), sem("totals12")
        folded, power_done, root_done = sem("folded"), sem("power_done"), sem("root_done")
        gain_step = sem("gain_step")
        z_done, z_turned = sem("z_done"), sem("z_turned")
        bn_step, mv_done, sd_done = sem("bn_step"), sem("mv_done"), sem("sd_done")
        rs_done, nb_done = sem("rs_done"), sem("nb_done")
        moments_cleared = sem("moments_cleared")
        y_done = sem("y_done")
        y_out = [sem(f"y_out{s}") for s in range(2)]

        def features(row, bank, h):
            cols = slice(h * C, (h + 1) * C)
            return ((row[:, 0:C], bank[:, 0, cols]),
                    (row[:, C:F].rearrange("p (c k) -> p k c", k=3), bank[:, 1:4, cols]))

        block = ctx.enter_context(nc.Block())

        @block.sync
        def _(sp):
            def load(i, s):
                n = 2 * i + s
                at_least(sp, turned, n - 1)
                for h in range(2):
                    sp.dma_start(rows[s][:, :, h, :],
                                 sums_dram[bass.ds(n * P + h * sz.half, P), :].rearrange("p (j c) -> p j c", j=J)).then_inc(rows_in[s], 16)

            load(0, 0)
            load(0, 1)
            sp.dma_start(x[:, :, :], x_cm).then_inc(x_in, 16)
            for n in (2, 3):
                load(n // 2, n % 2)
            with sp.Fori(2, N // 2) as i:
                for s in range(2):
                    load(i, s)

            def store(i, s):
                n = 2 * i + s
                sp.wait_ge(y_done, n + 1)
                for h in range(2):
                    sp.dma_start(out[bass.ds(n * P + h * sz.half, P), :],
                                 y[s][:, h, :]).then_inc(y_out[s], 16)

            with sp.Fori(0, N // 2) as i:
                for s in range(2):
                    store(i, s)
            for s in range(2):
                sp.wait_ge(y_out[s], 32 * (N // 2))

        @block.tensor
        def _(pe):
            def turn(i, s):
                n = 2 * i + s
                pe.wait_ge(rows_in[s], 32 * (i + 1))
                at_least(pe, turned_out, n - 1)
                for j in range(J):
                    last = nc.tensor.transpose(tr_ps[s][:, j, :], rows[s][:, j, :, :], identity[:, :])
                last.then_inc(turned, 1)

            def linear(n, s):
                pe.wait_ge(turned_out, n + 1)
                at_least(pe, a_out, 2 * (n - 1))
                nc.tensor.matmul(a_ps[s][:, 0, :], w_lin[:, 0, :], msg_t[s][:, 0, :], start=True, stop=True)
                nc.tensor.matmul(a_ps[s][:, 1:4, :], w_lin[:, 1, :], msg_t[s][:, 1:4, :],
                                 start=True, stop=True).then_inc(a_done, 1)

            def back(n, s):
                at_least(pe, o_out, n - 1)
                here = x[:, :, bass.ds(n * P, P)]
                nc.tensor.matmul(o_ps[s][:, 0, :], w_self[:, 0, :], here[:, 0, :], start=True, stop=False)
                pe.wait_ge(b_done, 2 * n + 2)
                nc.tensor.matmul(o_ps[s][:, 0, :], w_back[:, 0, :], b[s][:, 0, :], start=False, stop=True)
                nc.tensor.matmul(o_ps[s][:, 1:4, :], w_self[:, 1, :], here[:, 1:4, :], start=True, stop=False)
                nc.tensor.matmul(o_ps[s][:, 1:4, :], w_back[:, 1, :], b[s][:, 1:4, :],
                                 start=False, stop=True).then_inc(o_done, 1)

            def forward(i, s):
                n = 2 * i + s
                static = isinstance(n, int)
                if not (static and n + 2 >= N):
                    turn(i + 1, s)
                if not (static and n + 1 >= N):
                    linear(n + 1, 1 - s)
                back(n, s)

            turn(0, 0)
            turn(0, 1)
            linear(0, 0)
            pe.wait_ge(x_in, 16)
            in_pairs(pe, forward, N)

            pe.wait_ge(total0, 1)
            nc.tensor.matmul(stat_ps[:, 0:1], fold_halves[:, :], total[:, 0:1], start=True, stop=True).then_inc(folded, 1)
            pe.wait_ge(totals12, 3)
            pe.wait_ge(mean_done, 1)
            nc.tensor.matmul(stat_ps[:, 1:3], fold_halves[:, :], total[:, 1:3], start=True, stop=True).then_inc(folded, 1)

            def turn_back(i, s):
                n = 2 * i + s
                pe.wait_ge(z_done, 2 * n + 2)
                at_least(pe, y_done, n - 1)
                for j in range(J):
                    last = nc.tensor.transpose(tr_ps[s][:, j, :], z[s][:, j, :], identity[:, :])
                last.then_inc(z_turned, 1)

            in_pairs(pe, turn_back, N)

        @block.scalar
        def _(act):
            def turn_copy(n, s):
                act.wait_ge(turned, n + 1)
                at_least(act, a_done, n - 1)
                nc.scalar.activation(msg_t[s][:, :, :], tr_ps[s][:, :, :], ACT.Copy).then_inc(turned_out, 1)

            def a_copy(n, s):
                act.wait_ge(a_done, n + 1)
                at_least(act, b_done, 2 * (n - 1))
                nc.scalar.activation(a[s][:, :, :], a_ps[s][:, :, :], ACT.Copy).then_inc(a_out, 1)
                nc.scalar.activation(a_sq[s][:, :, :], a_ps[s][:, 1:4, :], ACT.Square).then_inc(a_out, 1)

            def forward(i, s):
                n = 2 * i + s
                static = isinstance(n, int)
                if not (static and n + 2 >= N):
                    turn_copy(n + 2, s)
                if not (static and n + 1 >= N):
                    a_copy(n + 1, 1 - s)
                act.wait_ge(o_done, n + 1)
                nc.scalar.activation(o[:, :, bass.ds(n * P, P)], o_ps[s][:, :, :], ACT.Copy).then_inc(o_out, 1)

            turn_copy(0, 0)
            turn_copy(1, 1)
            a_copy(0, 0)
            in_pairs(act, forward, N)

            act.wait_ge(o_out, N)
            nc.scalar.activation(squares[:, :, :], o[:, 1:4, :], ACT.Square,
                                 accum_out=total[:, 2:3]).then_inc(totals12, 1)
            act.wait_ge(mean_done, 1)
            act.wait_ge(totals12, 1)
            for h, real in enumerate((sz.half, sz.second)):
                part = slice(h * C, (h + 1) * C)
                nc.scalar.activation(squares[part, 0, 0:real], o[part, 0, 0:real], ACT.Square,
                                     bias=mean[part, 1:2], accum_out=total[part, 1:2]).then_inc(totals12, 1)
            act.wait_ge(power_done, 2)
            nc.scalar.activation(root[:, :], power[:, :], ACT.Sqrt, bias=eps_col[:, 0:1]).then_inc(root_done, 1)

            def finish(i, s):
                n = 2 * i + s
                act.wait_ge(mv_done, 2 * n + 2)
                nc.scalar.activation(sd[s][:, :], mv[s][:, :, 1], ACT.Sqrt, bias=eps_col[:, 0:1]).then_inc(sd_done, 1)
                act.wait_ge(nb_done, n + 1)
                at_least(act, y_out[s], 32 * i)
                for h in range(2):
                    for to, frm in features(y[s][:, h, :], tr_ps[s], h):
                        last = nc.scalar.activation(to, frm, ACT.Identity, bias=nb[s][:, h:h + 1],
                                                    scale=rs[s][:, h:h + 1])
                last.then_inc(y_done, 1)

            in_pairs(act, finish, N)

        @block.vector
        def _(dve):
            def contract(i, s):
                n = 2 * i + s
                a0 = a[s][:, 0, :]
                dve.wait_ge(a_out, 2 * n + 2)
                at_least(dve, o_done, n - 1)
                nc.vector.tensor_tensor(vv[s][:, :], a_sq[s][:, 0, :], a_sq[s][:, 1, :], ALU.add).then_inc(vv_done, 1)
                nc.vector.tensor_scalar(acc0[:, :], a0, poly0[:, 3:4], poly0[:, 1:2], ALU.mult, ALU.add)
                nc.vector.tensor_scalar(acc1[:, :], a0, poly1[:, 2:3], poly1[:, 1:2], ALU.mult, ALU.add).then_inc(poly_step, 1)
                dve.wait_ge(vv_done, 2 * n + 1)
                nc.vector.tensor_tensor(vv[s][:, :], vv[s][:, :], a_sq[s][:, 2, :], ALU.add).then_inc(vv_done, 1)
                dve.wait_ge(poly_step, 4 * n + 1)
                nc.vector.tensor_tensor(acc0[:, :], acc0[:, :], a0, ALU.mult)
                nc.vector.tensor_tensor(acc1[:, :], acc1[:, :], a0, ALU.mult).then_inc(poly_step, 1)
                dve.wait_ge(poly_step, 4 * n + 2)
                dve.wait_ge(vv_done, 2 * n + 2)
                nc.vector.scalar_tensor_tensor(out=acc0[:, :], in0=vv[s][:, :], scalar=poly0[:, 4:5], in1=acc0[:, :],
                                               op0=ALU.mult, op1=ALU.add)
                nc.vector.scalar_tensor_tensor(out=acc1[:, :], in0=vv[s][:, :], scalar=poly1[:, 3:4], in1=acc1[:, :],
                                               op0=ALU.mult, op1=ALU.add).then_inc(poly_step, 1)
                dve.wait_ge(poly_step, 4 * n + 3)
                nc.vector.scalar_tensor_tensor(out=acc0[:, :], in0=acc0[:, :], scalar=poly0[:, 0:1], in1=a0,
                                               op0=ALU.add, op1=ALU.mult).then_inc(poly_step, 1)
                nc.vector.scalar_tensor_tensor(out=b[s][:, 1:4, :],
                                               in0=acc1[:, :].unsqueeze(1).to_broadcast([P, 3, P]),
                                               scalar=poly1[:, 0:1], in1=a[s][:, 1:4, :],
                                               op0=ALU.add, op1=ALU.mult).then_inc(b_done, 1)
                dve.wait_ge(poly_step, 4 * n + 4)
                nc.vector.scalar_tensor_tensor(out=b[s][:, 0, :], in0=vv[s][:, :], scalar=poly0[:, 2:3], in1=acc0[:, :],
                                               op0=ALU.mult, op1=ALU.add).then_inc(b_done, 1)
                dve.wait_ge(b_done, 2 * n + 2)

            in_pairs(dve, contract, N)

            nodes = float(sz.nodes)
            dve.wait_ge(o_out, N)
            nc.vector.tensor_reduce(total[:, 0:1], o[:, 0, :], AX.X, ALU.add).then_inc(total0, 1)
            dve.wait_ge(folded, 1)
            nc.vector.tensor_scalar(mean[:, 0:1], stat_ps[:, 0:1], 1.0 / nodes, None, ALU.mult)
            nc.vector.tensor_scalar(mean[:, 1:2], stat_ps[:, 0:1], -1.0 / nodes, None, ALU.mult).then_inc(mean_done, 1)
            dve.wait_ge(folded, 2)
            nc.vector.tensor_scalar(power[:, 0:1], stat_ps[:, 1:2], 1.0 / nodes, None, ALU.mult).then_inc(power_done, 1)
            nc.vector.tensor_scalar(power[:, 1:2], stat_ps[:, 2:3], 1.0 / (3 * nodes), None, ALU.mult).then_inc(power_done, 1)
            dve.wait_ge(root_done, 1)
            nc.vector.reciprocal(gain[:, 0:2], root[:, :]).then_inc(gain_step, 1)
            dve.wait_ge(gain_step, 1)
            nc.vector.tensor_tensor(gain[:, 2:3], gain[:, 0:1], affine[:, 0:1], ALU.mult)
            nc.vector.tensor_tensor(gain[:, 3:4], gain[:, 1:2], affine[:, 2:3], ALU.mult).then_inc(gain_step, 1)
            dve.wait_ge(gain_step, 2)
            nc.vector.tensor_tensor(shift[:, 0:1], mean[:, 1:2], gain[:, 2:3], ALU.mult).then_inc(gain_step, 1)
            dve.wait_ge(gain_step, 3)
            nc.vector.tensor_tensor(shift[:, 1:2], shift[:, 0:1], affine[:, 1:2], ALU.add).then_inc(gain_step, 1)
            dve.wait_ge(gain_step, 4)
            nc.vector.tensor_scalar(x[:, 0, :], x[:, 0, :], shift[:, 1:2], None, ALU.add).then_inc(gain_step, 1)
            dve.wait_ge(gain_step, 5)

            def residual(n, s):
                at_least(dve, z_turned, n - 1)
                at = bass.ds(n * P, P)
                for j, k, g in ((0, 1, 2), (1, 4, 3)):
                    nc.vector.scalar_tensor_tensor(out=z[s][:, j:k, :], in0=o[:, j:k, at], scalar=gain[:, g:g + 1],
                                                   in1=x[:, j:k, at], op0=ALU.mult, op1=ALU.add).then_inc(z_done, 1)

            def moments(n, s):
                dve.wait_ge(z_turned, n + 1)
                at_least(dve, sd_done, n - 1)
                for h in range(2):
                    nc.vector.bn_stats(bn[s][:, h, :], tr_ps[s][:, :, h * C:(h + 1) * C]).then_inc(bn_step, 1)
                for h in range(2):
                    dve.wait_ge(bn_step, 2 * n + h + 1)
                    clear(dve, moments_cleared)
                    nc.vector.bn_aggr(mv[s][:, h, :], bn[s][:, h, :]).then_inc(mv_done, 1)

            def finish(n, s):
                dve.wait_ge(sd_done, n + 1)
                at_least(dve, y_done, n - 1)
                nc.vector.reciprocal(rs[s][:, :], sd[s][:, :]).then_inc(rs_done, 1)
                dve.wait_ge(rs_done, n + 1)
                nc.vector.scalar_tensor_tensor(out=nb[s][:, :], in0=mv[s][:, :, 0], scalar=-1.0, in1=rs[s][:, :],
                                               op0=ALU.mult, op1=ALU.mult).then_inc(nb_done, 1)

            def step(i, s):
                n = 2 * i + s
                static = isinstance(n, int)
                residual(n, s)
                if not (static and n < 1):
                    moments(n - 1, 1 - s)
                    finish(n - 1, 1 - s)

            in_pairs(dve, step, N)
            dve.wait_ge(z_turned, N)
            moments(N - 1, 1)
            finish(N - 1, 1)


_WEIGHTS = ("W_up0", "W_up1", "M1", "M2", "M3", "M4", "W_lin0", "W_lin1", "Wsc0", "Wsc1", "Wc0", "Wc1",
            "WB0", "WB1", "gamma0", "beta0", "gamma1")


def kernel(x, src, dst, edge_attr_16, edge_attr_4, **layer):
    import numpy as np
    import concourse.bacc as bacc
    from concourse.bass_utils import run_bass_kernel_spmd as run

    x, src, dst, rbf, sh = (np.asarray(v) for v in (x, src, dst, edge_attr_16, edge_attr_4))
    sz = Shapes(x.shape[0], src.shape[0])
    more = sz.padded_edges - sz.edges
    xp = np.pad(x, ((0, sz.rows - sz.nodes), (0, 0)))
    comps = np.concatenate([xp[:, None, :C], xp[:, C:].reshape(sz.rows, C, 3).transpose(0, 2, 1)], axis=1)
    x_cm = comps.reshape(2, sz.half, J, C).transpose(0, 3, 2, 1).reshape(P, J, sz.half)
    src_p = np.pad(src, (0, more), mode="edge").reshape(sz.groups, TG, P)
    dst_p = np.pad(dst, (0, more), mode="edge").reshape(sz.groups, TG, P)
    sh_p = np.pad(sh, ((0, more), (0, 0))).reshape(sz.groups, TG, P, 4)
    rbf_p = np.pad(rbf, ((0, more), (0, 0))).reshape(sz.groups, 2, 4 * P, 16)
    arrays = {
        "x_cm": x_cm,
        "src_idx": src_p.transpose(0, 2, 1).reshape(sz.groups * P, TG),
        "dst_pt": dst_p.transpose(2, 0, 1).reshape(P, sz.tiles),
        "dst_rows": dst_p.reshape(sz.groups, GE),
        "first_dst": dst_p[:, 0, 0].reshape(1, sz.groups),
        "sh_in": sh_p.transpose(0, 2, 1, 3).reshape(sz.groups * P, TG * 4),
        "rbf_in": rbf_p.transpose(0, 1, 3, 2).reshape(sz.groups * 32, 4 * P),
    }
    for name in _WEIGHTS:
        arrays[name] = np.asarray(layer["L0_gnn_" + name])
    arrays = {name: np.ascontiguousarray(a) for name, a in arrays.items()}
    nc = bacc.Bacc("TRN2", target_bir_lowering=False, num_devices=1)
    aps = {name: nc.dram_tensor(name + "_dram", a.shape, mybir.dt.from_np(a.dtype), kind="ExternalInput").ap()
           for name, a in arrays.items()}
    out = nc.dram_tensor("out_dram", (sz.rows, F), F32, kind="ExternalOutput").ap()
    weights = {name: aps.pop(name) for name in _WEIGHTS}
    build(nc, aps["x_cm"], aps["src_idx"], aps["dst_pt"], aps["dst_rows"], aps["first_dst"], aps["sh_in"],
          aps["rbf_in"], weights, out, sz)
    result = run(nc, [{name + "_dram": a for name, a in arrays.items()}], core_ids=[0])
    return result.results[0]["out_dram"][:sz.nodes]
```

```python
from contextlib import ExitStack

import concourse.bass as bass
from concourse import mybir
from concourse.alu_op_type import AluOpType as ALU

ACT = mybir.ActivationFunctionType
AX = mybir.AxisListType
F32 = mybir.dt.float32
I32 = mybir.dt.int32
BF16 = mybir.dt.bfloat16

P = 128
C = 64
J = 4
F = J * C
TG = 8
GE = TG * P
SLOTS = 4
WINDOW = 80
EPS = 1e-5


WEIGHT_PARTS = (("w_lin", 2 * P), ("w_self", 2 * P), ("w_back", 2 * P), ("w_m1", P), ("w_m2", P), ("w_m3", P),
                ("w_m4", 2 * F), ("poly0", 5), ("poly1", 4), ("affine", 3))
WEIGHT_COLUMNS = sum(width for _name, width in WEIGHT_PARTS)


class Shapes:

    def __init__(self, nodes, edges):
        self.nodes = nodes
        self.edges = edges
        self.pairs = 2 * (-(-nodes // (4 * P)))
        self.half = self.pairs * P
        self.rows = 2 * self.half
        self.second = nodes - self.half
        self.groups = SLOTS * (-(-edges // (GE * SLOTS)))
        self.tiles = self.groups * TG
        self.padded_edges = self.groups * GE
        self.dump = self.rows
        self.sum_rows = self.rows + P


def at_least(engine, semaphore, value):
    if isinstance(value, int) and value <= 0:
        return
    engine.wait_ge(semaphore, value)


def clear(engine, passed):
    engine.sem_inc(passed, 1)


def run_steps(engine, step, steps, extra):
    first = 2 * SLOTS
    last = steps - SLOTS
    for g in range(min(first, steps)):
        step(g // SLOTS, g % SLOTS)
    if last > first:
        with engine.Fori(first // SLOTS, last // SLOTS) as i:
            for u in range(SLOTS):
                step(i, u)
    for g in range(max(last, first), steps + extra):
        step(g // SLOTS, g % SLOTS)


def in_pairs(engine, step, count, begin=0):
    bodies = count // 2
    for n in range(begin, min(4, count)):
        step(n // 2, n % 2)
    if bodies > 3:
        with engine.Fori(2, bodies - 1) as i:
            for s in range(2):
                step(i, s)
    for n in range(max(4, count - 2), count):
        step(n // 2, n % 2)


def slot_of(i, u, ahead=0):
    return i + (u + ahead) // SLOTS, (u + ahead) % SLOTS


def build(nc, x_cm, src_idx, dst_pt, dst_rows, first_dst, sh_in, rbf_in, w_up_dram, table_dram, out, sizes):
    sz = sizes
    G = sz.groups
    with ExitStack() as top:
        def sem(name):
            return top.enter_context(nc.semaphore(name))

        def keep(name, shape, dt=F32):
            return top.enter_context(nc.sbuf_tensor(name, shape, dt))

        up_dram = nc.dram_tensor("up_rows", (sz.rows, F), F32, kind="Internal").ap()
        sums_dram = nc.dram_tensor("message_sums", (sz.sum_rows, F), F32, kind="Internal").ap()

        identity = keep("identity", [P, P])
        fold_halves = keep("fold_halves", [P, P])
        x = keep("x", [P, J, sz.half])
        w_up = keep("w_up", [P, 2, P])
        table = keep("table", [P, WEIGHT_COLUMNS])
        at = 0
        parts = {}
        for name, width in WEIGHT_PARTS:
            parts[name] = table[:, at:at + width]
            at += width
        w_m4 = parts["w_m4"]
        zeros = keep("zeros", [P, F])
        eps_col = keep("eps_col", [P, 1])
        lane_row = keep("lane_row", [P, P])
        lane_col = keep("lane_col", [P, 1])
        rel = keep("rel", [P, sz.tiles])
        base_f = keep("base_f", [P, G])
        window_rows = keep("window_rows", [P, G], I32)
        lower = keep("lower", [P, P])
        misfit = keep("misfit", [1, 1], I32)
        table_in = sem("table_in")
        zeroed = sem("zeroed")

        with ExitStack() as ctx:
            def sb(name, shape, dt=F32):
                return ctx.enter_context(nc.sbuf_tensor(name, shape, dt))

            lane_row_i = sb("lane_row_i", [P, P], I32)
            lane_col_i = sb("lane_col_i", [P, 1], I32)
            ones = sb("ones", [P, P])
            dst_i = sb("dst_i", [P, sz.tiles], I32)
            base_i = sb("base_i", [P, G], I32)
            CH = 2
            x_ring = [sb(f"x_ring{s}", [P, J, CH * P]) for s in range(2)]
            rows_f = sb("rows_f", [P, G])
            far = sb("far", [P, 4])
            up_sb = [sb(f"up_sb{s}", [P, CH, 2, J, C]) for s in range(2)]
            up_ps = [[ctx.enter_context(nc.psum_tensor(f"up_ps{s}_{q}", [P, J, 2, C], F32))
                      for q in range(CH)] for s in range(2)]
            count_ps = ctx.enter_context(nc.psum_tensor("count_ps", [P, 1], F32))

            w_up_in = sem("p1_w_up_in")
            dst_in = sem("p1_dst_in")
            x_in = [sem(f"p1_x_in{s}") for s in range(2)]
            up_done = sem("p1_up_done")
            x_kept = sem("p1_x_kept")
            copied = sem("p1_copied")
            up_out = [sem(f"p1_up_out{s}") for s in range(2)]
            patterns = sem("p1_patterns")
            dve_step = sem("p1_dve_step")
            far_made = sem("p1_far_made")
            counted = sem("p1_counted")

            chunks = sz.pairs // CH

            def by_chunk(engine, step, begin=0):
                in_pairs(engine, step, chunks // 2 * 2, begin)
                if chunks % 2:
                    step(chunks // 2, 0)

            block = ctx.enter_context(nc.Block())

            @block.sync
            def _(sp):
                sp.dma_start(w_up[:, :, :].rearrange("p v c -> p (v c)"), w_up_dram).then_inc(w_up_in, 16)

                def load(i, s):
                    k = 2 * i + s
                    at_least(sp, up_done, CH * (k - 1))
                    at_least(sp, x_kept, k - 1)
                    sp.dma_start(x_ring[s][:, :, :],
                                 x_cm[:, :, bass.ds(k * (CH * P), CH * P)]).then_inc(x_in[s], 16)

                load(0, 0)
                load(0, 1)
                sp.dma_start(dst_i[:, :], dst_pt).then_inc(dst_in, 16)
                sp.dma_start(base_i[:, :], first_dst.to_broadcast([P, G])).then_inc(dst_in, 16)
                sp.dma_start(table[:, :], table_dram).then_inc(table_in, 16)
                by_chunk(sp, load, 2)
                for s in range(2):
                    sp.wait_ge(up_out[s], 32 * ((chunks + 1 - s) // 2))

            @block.gpsimd
            def _(pool):
                nc.gpsimd.memset(identity[:, :], 0.0).then_inc(patterns, 1)
                nc.gpsimd.memset(lower[:, :], 1.0).then_inc(patterns, 1)
                nc.gpsimd.iota(lane_row_i[:, :], [[1, P]], base=0, channel_multiplier=0).then_inc(patterns, 1)
                nc.gpsimd.iota(lane_col_i[:, :], [[0, 1]], base=0, channel_multiplier=1).then_inc(patterns, 1)
                pool.wait_ge(patterns, 4)
                nc.gpsimd.affine_select(out=identity[:, :], in_=identity[:, :], compare_op=ALU.not_equal,
                                        fill=1.0, base=0, pattern=[[-1, P]],
                                        channel_multiplier=1).then_inc(patterns, 1)
                nc.gpsimd.affine_select(out=lower[:, :], in_=lower[:, :], compare_op=ALU.is_gt,
                                        fill=0.0, base=0, pattern=[[-1, P]],
                                        channel_multiplier=1).then_inc(patterns, 1)

            @block.scalar
            def _(act):
                def project(i, s):
                    k = 2 * i + s
                    at_least(act, up_out[s], 32 * i)
                    for q in range(CH):
                        act.wait_ge(up_done, CH * k + q + 1)
                        nc.scalar.activation(up_sb[s][:, q, :, :, :].rearrange("p h j c -> p j h c"),
                                             up_ps[s][q][:, :, :, :], ACT.Copy).then_inc(copied, 1)
                    act.wait_ge(copied, CH * (k + 1))
                    for h in range(2):
                        act.dma_start(
                            up_dram[bass.ds(k * (CH * P) + h * sz.half, CH * P), :]
                            .rearrange("(q p) f -> p q f", p=P),
                            up_sb[s][:, :, h, :, :].rearrange("p q j c -> p q (j c)"),
                        ).then_inc(up_out[s], 16)

                by_chunk(act, project)

            @block.vector
            def _(dve):
                nc.vector.memset(zeros[:, :], 0.0)
                nc.vector.memset(ones[:, :], 1.0)
                nc.vector.memset(eps_col[:, :], EPS).then_inc(dve_step, 1)

                def keep_nodes(i, s):
                    k = 2 * i + s
                    dve.wait_ge(x_in[s], 16 * (i + 1))
                    nc.vector.tensor_copy(x[:, :, bass.ds(k * (CH * P), CH * P)],
                                          x_ring[s][:, :, :]).then_inc(x_kept, 1)

                def patterns_and_fold():
                    dve.wait_ge(patterns, 6)
                    nc.vector.tensor_copy(lane_row[:, :], lane_row_i[:, :])
                    nc.vector.tensor_copy(lane_col[:, :], lane_col_i[:, :])
                    for h in range(2):
                        cols = slice(h * C, (h + 1) * C)
                        nc.vector.tensor_tensor(fold_halves[:, cols], identity[:, 0:C], identity[:, C:P], ALU.add)

                def relative_destinations():
                    dve.wait_ge(dst_in, 32)
                    nc.vector.tensor_copy(base_f[:, :], base_i[:, :]).then_inc(dve_step, 1)
                    nc.vector.tensor_tensor(rel[:, :].rearrange("p (g t) -> p g t", t=TG),
                                            dst_i[:, :].rearrange("p (g t) -> p g t", t=TG),
                                            base_i[:, :].unsqueeze(2).to_broadcast([P, G, TG]), ALU.subtract)
                    dve.wait_ge(dve_step, 2)
                    nc.vector.tensor_scalar(rows_f[:, :], base_f[:, :], lane_col[:, 0:1], None,
                                            ALU.add).then_inc(dve_step, 1)
                    dve.wait_ge(dve_step, 3)
                    nc.vector.tensor_copy(window_rows[:, :], rows_f[:, :])

                def find_misfits():
                    nc.vector.tensor_reduce(far[:, 0:1], rel[:, :], AX.X, ALU.max)
                    nc.vector.tensor_reduce(far[:, 1:2], rel[:, :], AX.X, ALU.min).then_inc(dve_step, 1)
                    dve.wait_ge(dve_step, 4)
                    nc.vector.tensor_scalar(far[:, 2:3], far[:, 0:1], float(WINDOW), None, ALU.is_ge)
                    nc.vector.tensor_scalar(far[:, 3:4], far[:, 1:2], 0.0, None, ALU.is_lt).then_inc(dve_step, 1)
                    dve.wait_ge(dve_step, 5)
                    nc.vector.tensor_tensor(far[:, 0:1], far[:, 2:3], far[:, 3:4], ALU.max).then_inc(far_made, 1)

                def scale_dot_weights():
                    dve.wait_ge(table_in, 16)
                    for h in range(2):
                        dots = w_m4[:, h * F + 2 * C:h * F + 3 * C]
                        nc.vector.tensor_scalar(dots, dots, float(3.0 ** -0.5), None, ALU.mult).then_inc(dve_step, 1)
                    dve.wait_ge(dve_step, 7)

                stages = (patterns_and_fold, relative_destinations, find_misfits, scale_dot_weights)
                for k, stage in enumerate(stages):
                    if k < chunks // 2 * 2:
                        keep_nodes(k // 2, k % 2)
                    stage()
                by_chunk(dve, keep_nodes, len(stages))
                dve.wait_ge(x_kept, chunks)
                dve.wait_ge(counted, 1)
                nc.vector.tensor_copy(misfit[:, :], count_ps[0:1, :]).then_inc(dve_step, 1)
                dve.wait_ge(dve_step, 8)

            @block.tensor
            def _(pe):
                pe.wait_ge(w_up_in, 16)

                def project(i, s):
                    k = 2 * i + s
                    pe.wait_ge(x_in[s], 16 * (i + 1))
                    at_least(pe, copied, CH * (k - 1))
                    for q in range(CH):
                        for j in range(J):
                            last = nc.tensor.matmul(up_ps[s][q][:, j, :, :],
                                                    x_ring[s][:, j, q * P:(q + 1) * P],
                                                    w_up[:, min(j, 1), :], start=True, stop=True)
                        last.then_inc(up_done, 1)

                by_chunk(pe, project)
                pe.wait_ge(far_made, 1)
                nc.tensor.matmul(count_ps[:, :], ones[:, :], far[:, 0:1], start=True, stop=True).then_inc(counted, 1)

        for general in (False, True):
            edges(nc, sz, general, up_dram, sums_dram, src_idx, dst_rows, sh_in, rbf_in,
                  parts, zeros, zeroed, lane_row, lane_col, lower, rel, base_f, window_rows, misfit)

        node_phase(nc, sz, x, sums_dram, out, identity, fold_halves, parts, eps_col)


def edges(nc, sz, general, up_dram, sums_dram, src_idx, dst_rows, sh_in, rbf_in,
          parts, zeros, zeroed, lane_row, lane_col, lower, rel, base_f, window_rows, misfit):
    G = sz.groups
    tag = "any_" if general else "win_"
    reduce_lag = 2
    copy_lag = 2 if general else 3
    scatter_lag = 5 if general else 6
    rows_lag = SLOTS
    copies = 2 if general else 1
    per_group = TG if general else 1
    window = P if general else WINDOW
    w_m1, w_m2, w_m3, w_m4 = parts["w_m1"][0:32, :], parts["w_m2"], parts["w_m3"], parts["w_m4"]
    with ExitStack() as ctx:
        def sb(name, shape, dt=F32):
            return ctx.enter_context(nc.sbuf_tensor(tag + name, shape, dt))

        def ps(name, shape):
            return ctx.enter_context(nc.psum_tensor(tag + name, shape, F32))

        def sem(name):
            return ctx.enter_context(nc.semaphore(tag + name))

        idx = [sb(f"idx{s}", [P, TG], I32) for s in range(SLOTS)]
        sh = [sb(f"sh{s}", [P, TG, 4]) for s in range(SLOTS)]
        rbf = [sb(f"rbf{s}", [32, 4 * P]) for s in range(SLOTS)]
        X = [sb(f"X{s}", [P, TG, C + F]) for s in range(SLOTS)]
        hid1 = sb("hid1", [P, 4 * P])
        hid2 = sb("hid2", [P, 4 * P])
        hid3 = [sb(f"hid3_{s}", [P, 4 * P]) for s in range(2)]
        scaled = [sb(f"scaled{s}", [P, TG, 2, C]) for s in range(2)]
        dots = [sb(f"dots{s}", [P, TG, 3, C]) for s in range(2)]
        dot01 = sb("dot01", [P, TG, C])
        part = sb("part", [P, TG, 5, C])
        msg = [sb(f"msg{s}", [P, TG, J, C]) for s in range(2)]
        hot = [sb(f"hot{s}", [P, TG, window]) for s in range(2)]
        sums = [sb(f"sums{s}", [window, F]) for s in range(2)]
        sums_at = [sb(f"sums_at{s}", [window, 1], I32) for s in range(2 if general else SLOTS)]
        if general:
            drow_i = [sb(f"drow_i{s}", [P, TG * P], I32) for s in range(SLOTS)]
            drow_f = sb("drow_f", [P, TG, P])
            before = sb("before", [P, TG, P], BF16)
            dst = sb("dst", [P, TG])
            earlier = sb("earlier", [P, TG])
            spare = sb("spare", [P, TG])
            rows_i = [sb(f"rows_i{s}", [P, TG], I32) for s in range(2)]
        hid_ps = [ps(f"hid_ps{b}", [P, 4 * P]) for b in range(2)]
        tpw_ps = [ps(f"tpw_ps{b}", [P, 2, J, C]) for b in range(4)]
        sum_ps = [ps(f"sum_ps{b}", [window, F]) for b in range(2)]

        loaded = [sem(f"loaded{s}") for s in range(SLOTS)]
        gathered = [sem(f"gathered{s}") for s in range(SLOTS)]
        mm1, mm2, mm3 = sem("mm1"), sem("mm2"), sem("mm3")
        act1, act2, act3 = sem("act1"), sem("act2"), sem("act3")
        mm4 = sem("mm4")
        scaled_done = sem("scaled_done")
        dots_done = sem("dots_done")
        dot01_done, u_done = sem("dot01_done"), sem("u_done")
        part_done = sem("part_done")
        hot_done = sem("hot_done")
        cross_done = sem("cross_done")
        own_done = sem("own_done")
        msg_done = sem("msg_done")
        summed = sem("summed")
        sums_out = sem("sums_out")
        rows_in = [sem(f"rows_in{s}") for s in range(SLOTS)]
        scattered = sem("scattered")
        gathers_cleared, scatters_cleared = sem("gathers_cleared"), sem("scatters_cleared")
        rank_step = sem("rank_step")

        enter = ctx.enter_context(nc.Block())
        block = enter
        n_in = 4 if general else 3

        def chosen(engine):
            count = engine.value_load(misfit[0:1, 0:1], min_val=0, max_val=P)
            return engine.If(count > 0 if general else count < 1)

        @block.sync
        def _(sp):
            def step(i, u):
                g = SLOTS * i + u
                static = isinstance(g, int)
                if not (static and g >= G):
                    load(g, i, u)
                if static and g < SLOTS:
                    per = sz.sum_rows // P
                    part = slice(g * per // SLOTS, (g + 1) * per // SLOTS)
                    sp.dma_start(sums_dram.rearrange("(p r) f -> p r f", p=P)[:, part, :],
                                 zeros[:, :].unsqueeze(1).to_broadcast([P, part.stop - part.start, F]),
                                 ).then_inc(zeroed, 16)
                if not general and not (static and not 0 <= g - rows_lag < G):
                    at_least(sp, scattered, 16 * (g - rows_lag - SLOTS + 1))
                    sp.dma_start(sums_at[u][:, :],
                                 window_rows[0:window, bass.ds(g - rows_lag, 1)]).then_inc(rows_in[u], 16)

            def load(g, i, u):
                at_least(sp, msg_done, g - SLOTS + 1)
                sp.dma_start(rbf[u][:, :], rbf_in[bass.ds(g * 32, 32), :]).then_inc(loaded[u], 16)
                sp.dma_start(idx[u][:, :], src_idx[bass.ds(g * P, P), :]).then_inc(loaded[u], 16)
                sp.dma_start(sh[u][:, :, :].rearrange("p t k -> p (t k)"),
                             sh_in[bass.ds(g * P, P), :]).then_inc(loaded[u], 16)
                if general:
                    sp.dma_start(drow_i[u][:, :],
                                 dst_rows[bass.ds(g, 1), :].to_broadcast([P, GE])).then_inc(loaded[u], 16)

            with chosen(sp):
                run_steps(sp, step, G, 0 if general else rows_lag)
                sp.wait_ge(scattered, 16 * G * per_group)

        @block.gpsimd
        def _(pool):
            def step(i, u):
                g = SLOTS * i + u
                static = isinstance(g, int)
                if not (static and g >= G):
                    pool.wait_ge(loaded[u], 16 * n_in * (i + 1))
                    at_least(pool, msg_done, g - SLOTS + 1)
                    clear(pool, gathers_cleared)
                    for t in range(TG):
                        pool.indirect_dma_start(
                            out=X[u][:, t, C:C + F], out_offset=None, in_=up_dram[:, :],
                            in_offset=bass.IndirectOffsetOnAxis(ap=idx[u][:, t:t + 1], axis=0),
                        ).then_inc(gathered[u], 16)
                done = g - scatter_lag
                if static and not 0 <= done < G:
                    return
                before_i, before_u = slot_of(i, u, -scatter_lag)
                for t in range(per_group):
                    n = done * per_group + t
                    s = t % 2 if general else before_u % 2
                    at = sums_at[s if general else before_u]
                    pool.wait_ge(sums_out, copies * (n + 1))
                    if not general:
                        pool.wait_ge(rows_in[before_u], 16 * (before_i + 1))
                    if static and n == 0:
                        pool.wait_ge(zeroed, 16 * SLOTS)
                    at_least(pool, scattered, 16 * n)
                    clear(pool, scatters_cleared)
                    pool.indirect_dma_start(
                        out=sums_dram[:, :],
                        out_offset=bass.IndirectOffsetOnAxis(ap=at[:, 0:1], axis=0),
                        in_=sums[s][:, :], in_offset=None, compute_op=ALU.add,
                    ).then_inc(scattered, 16)

            with chosen(pool):
                run_steps(pool, step, G, scatter_lag)

        @block.tensor
        def _(pe):
            def layer1(i, u):
                g = SLOTS * i + u
                pe.wait_ge(loaded[u], 16 * n_in * (i + 1))
                at_least(pe, act2, g)
                nc.tensor.matmul(hid_ps[u % 2][:, :], w_m1[:, :], rbf[u][:, :],
                                 start=True, stop=True).then_inc(mm1, 1)

            def layer2(i, u):
                pe.wait_ge(act1, SLOTS * i + u + 1)
                nc.tensor.matmul(hid_ps[(u + 1) % 2][:, :], w_m2[:, :], hid1[:, :],
                                 start=True, stop=True).then_inc(mm2, 1)

            def layer3(i, u):
                pe.wait_ge(act2, SLOTS * i + u + 1)
                nc.tensor.matmul(hid_ps[u % 2][:, :], w_m3[:, :], hid2[:, :],
                                 start=True, stop=True).then_inc(mm3, 1)

            def layer4(g, u, q):
                if q == 0:
                    pe.wait_ge(act3, g + 1)
                at_least(pe, part_done, 4 * g - 4 + q + 1)
                nc.tensor.matmul(tpw_ps[q][:, :, :, :], hid3[u % 2][:, q * P:(q + 1) * P],
                                 w_m4[:, :], start=True, stop=True).then_inc(mm4, 1)

            def reduce_group(g, u):
                pe.wait_ge(hot_done, g + 1)
                pe.wait_ge(msg_done, g + 1)
                if not general:
                    at_least(pe, sums_out, g - 1)
                for t in range(TG):
                    n = g * TG + t
                    if general:
                        at_least(pe, sums_out, 2 * (n - 1))
                    b = t % 2 if general else u % 2
                    done = nc.tensor.matmul(sum_ps[b][:, :], hot[u % 2][:, t, :],
                                            msg[u % 2][:, t, :, :],
                                            start=general or t == 0, stop=general or t == TG - 1)
                    if general:
                        done.then_inc(summed, 1)
                if not general:
                    done.then_inc(summed, 1)

            def step(i, u):
                g = SLOTS * i + u
                static = isinstance(g, int)
                ni, nu = slot_of(i, u, 1)
                ahead = not (static and g + 1 >= G)
                here = not (static and g >= G)
                if ahead:
                    layer1(ni, nu)
                if here:
                    layer4(g, u, 0)
                    layer4(g, u, 1)
                if ahead:
                    layer2(ni, nu)
                if here:
                    layer4(g, u, 2)
                    layer4(g, u, 3)
                if ahead:
                    layer3(ni, nu)
                if not (static and g < reduce_lag):
                    reduce_group(g - reduce_lag, (u - reduce_lag) % SLOTS)

            with chosen(pe):
                layer1(0, 0)
                layer2(0, 0)
                layer3(0, 0)
                run_steps(pe, step, G, reduce_lag)

        @block.scalar
        def _(act):
            def silu(layer, i, u):
                g = SLOTS * i + u
                ready = (mm1, mm2, mm3)[layer]
                out = (hid1, hid2, hid3[u % 2])[layer]
                bank = hid_ps[(u + layer % 2) % 2]
                act.wait_ge(ready, g + 1)
                nc.scalar.activation(out[:, :], bank[:, :], ACT.Silu).then_inc((act1, act2, act3)[layer], 1)

            def scale_weights(g, u, q):
                if q == 0:
                    at_least(act, own_done, 2 * (g - 1))
                act.wait_ge(mm4, 4 * g + q + 1)
                for h in range(2):
                    t = q + 4 * h
                    done = nc.scalar.activation(scaled[u % 2][:, t, :, :], tpw_ps[q][:, h, 0:2, :],
                                                ACT.Copy, scale=sh[u][:, t, 0:1])
                done.then_inc(scaled_done, 1)

            def dot_products(i, u, tiles):
                g = SLOTS * i + u
                if tiles[0] == 0:
                    act.wait_ge(loaded[u], 16 * n_in * (i + 1))
                    act.wait_ge(gathered[u], 16 * TG * (i + 1))
                    at_least(act, u_done, g - 1)
                for t in tiles:
                    for k in range(3):
                        done = nc.scalar.activation(dots[u % 2][:, t, k, :],
                                                    X[u][:, t, (2 + k) * C:(3 + k) * C],
                                                    ACT.Copy, scale=sh[u][:, t, k + 1:k + 2])
                if tiles[-1] == TG - 1:
                    done.then_inc(dots_done, 1)

            def copy_sums(g, u):
                for t in range(per_group):
                    n = g * per_group + t
                    b = t % 2 if general else u % 2
                    act.wait_ge(summed, n + 1)
                    at_least(act, scattered, 16 * (n - 1))
                    nc.scalar.activation(sums[b][:, :], sum_ps[b][:, :], ACT.Copy).then_inc(sums_out, 1)
                    if general:
                        nc.scalar.copy(sums_at[b][:, :], rows_i[u % 2][:, t:t + 1]).then_inc(sums_out, 1)

            def step(i, u):
                g = SLOTS * i + u
                static = isinstance(g, int)
                ni, nu = slot_of(i, u, 1)
                ahead = not (static and g + 1 >= G)
                here = not (static and g >= G)
                if ahead:
                    silu(0, ni, nu)
                    dot_products(ni, nu, (0,))
                if here:
                    scale_weights(g, u, 0)
                    scale_weights(g, u, 1)
                if ahead:
                    dot_products(ni, nu, (1,))
                    silu(1, ni, nu)
                if here:
                    scale_weights(g, u, 2)
                if ahead:
                    dot_products(ni, nu, (2,))
                if here:
                    scale_weights(g, u, 3)
                if ahead:
                    silu(2, ni, nu)
                    dot_products(ni, nu, range(3, TG))
                if not (static and not 0 <= g - copy_lag < G):
                    copy_sums(g - copy_lag, (u - copy_lag) % SLOTS)

            with chosen(act):
                silu(0, 0, 0)
                silu(1, 0, 0)
                silu(2, 0, 0)
                dot_products(0, 0, range(TG))
                run_steps(act, step, G, copy_lag)

        @block.vector
        def _(dve):
            def make_hot(g, i, u):
                if general:
                    dve.wait_ge(loaded[u], 16 * n_in * (i + 1))
                at_least(dve, summed, per_group * (g - 1))
                here = rel[:, bass.ds(g * TG, TG)].unsqueeze(2).to_broadcast([P, TG, window])
                if general:
                    nc.vector.tensor_tensor(drow_f[:, :, :], drow_i[u][:, :].rearrange("p (t e) -> p t e", t=TG),
                                            base_f[:, bass.ds(g, 1)].unsqueeze(2).to_broadcast([P, TG, P]),
                                            ALU.subtract).then_inc(rank_step, 1)
                    dve.wait_ge(rank_step, 4 * g + 1)
                    lanes = drow_f[:, :, :]
                else:
                    lanes = lane_row[:, 0:window].unsqueeze(1).to_broadcast([P, TG, window])
                nc.vector.tensor_tensor(hot[u % 2][:, :, :], lanes, here, ALU.is_equal).then_inc(hot_done, 1)

            def rank(g, u):
                at_least(dve, sums_out, 2 * TG * (g - 1))
                dve.wait_ge(hot_done, g + 1)
                nc.vector.tensor_tensor(before[:, :, :], hot[u % 2][:, :, :],
                                        lower[:, :].unsqueeze(1).to_broadcast([P, TG, P]), ALU.mult)
                nc.vector.tensor_tensor(dst[:, :], rel[:, bass.ds(g * TG, TG)],
                                        base_f[:, bass.ds(g, 1)].to_broadcast([P, TG]),
                                        ALU.add).then_inc(rank_step, 1)
                dve.wait_ge(rank_step, 4 * g + 2)
                nc.vector.tensor_reduce(earlier[:, :], before[:, :, :], AX.X, ALU.max)
                nc.vector.tensor_scalar(spare[:, :], dst[:, :], -1.0,
                                        float(sz.dump), ALU.mult, ALU.add).then_inc(rank_step, 1)
                dve.wait_ge(rank_step, 4 * g + 3)
                nc.vector.tensor_scalar(earlier[:, :], earlier[:, :], 0.0, None, ALU.is_gt)
                nc.vector.tensor_scalar(spare[:, :], spare[:, :], lane_col[:, 0:1], None,
                                        ALU.add).then_inc(rank_step, 1)
                dve.wait_ge(rank_step, 4 * g + 4)
                nc.vector.tensor_tensor(spare[:, :], spare[:, :], earlier[:, :], ALU.mult).then_inc(cross_done, 1)
                dve.wait_ge(cross_done, 2 * g + 1)
                nc.vector.tensor_tensor(rows_i[u % 2][:, :], spare[:, :], dst[:, :], ALU.add)

            def sum_first(g, u):
                dve.wait_ge(dots_done, g + 1)
                nc.vector.tensor_tensor(dot01[:, :, :], dots[u % 2][:, :, 0, :], dots[u % 2][:, :, 1, :],
                                        ALU.add).then_inc(dot01_done, 1)

            def sum_last(g, u):
                dve.wait_ge(dot01_done, g + 1)
                nc.vector.tensor_tensor(X[u][:, :, 0:C], dot01[:, :, :], dots[u % 2][:, :, 2, :],
                                        ALU.add).then_inc(u_done, 1)

            def step(i, u):
                g = SLOTS * i + u
                static = isinstance(g, int)
                if static and g >= G:
                    return
                ahead = not (static and g + 1 >= G)
                nu = (u + 1) % SLOTS
                crosses = 2 * g + 2 if general else g + 1
                x = X[u]
                dve.wait_ge(u_done, g + 1)
                at_least(dve, msg_done, g)
                for q in range(4):
                    dve.wait_ge(scaled_done, 4 * g + q + 1)
                    nc.vector.tensor_tensor(
                        part[:, q::4, 0::4, :], tpw_ps[q][:, :, 2:4, :],
                        x[:, q::4, 0:2 * C].rearrange("p t (b c) -> p t b c", b=2), ALU.mult,
                    ).then_inc(part_done, 1)
                if general:
                    make_hot(g, i, u)
                    rank(g, u)
                at_least(dve, summed, per_group * (g - 1))
                nc.vector.tensor_tensor(msg[u % 2][:, :, 0, :], scaled[u % 2][:, :, 0, :],
                                        x[:, :, C:2 * C], ALU.mult).then_inc(own_done, 1)
                nc.vector.tensor_tensor(msg[u % 2][:, :, 1:4, :],
                                        scaled[u % 2][:, :, 1:2, :].to_broadcast([P, TG, 3, C]),
                                        x[:, :, 2 * C:5 * C].rearrange("p t (k c) -> p t k c", k=3),
                                        ALU.mult).then_inc(own_done, 1)
                dve.wait_ge(part_done, 4 * g + 4)
                nc.vector.tensor_tensor(part[:, :, 1:4, :], part[:, :, 4:5, :].to_broadcast([P, TG, 3, C]),
                                        sh[u][:, :, 1:4].unsqueeze(3).to_broadcast([P, TG, 3, C]),
                                        ALU.mult).then_inc(cross_done, 1)
                if ahead:
                    sum_first(g + 1, nu)
                dve.wait_ge(cross_done, crosses)
                dve.wait_ge(own_done, 2 * g + 2)
                nc.vector.tensor_tensor(msg[u % 2][:, :, :, :], msg[u % 2][:, :, :, :],
                                        part[:, :, 0:4, :], ALU.add).then_inc(msg_done, 1)
                if ahead:
                    sum_last(g + 1, nu)
                if not general:
                    make_hot(g, i, u)

            with chosen(dve):
                sum_first(0, 0)
                sum_last(0, 0)
                run_steps(dve, step, G, 0)


def node_phase(nc, sz, x, sums_dram, out, identity, fold_halves, parts, eps_col):
    N = sz.pairs
    w_lin, w_self, w_back = (parts[name].rearrange("p (v c) -> p v c", v=2)
                             for name in ("w_lin", "w_self", "w_back"))
    poly0, poly1, affine = parts["poly0"], parts["poly1"], parts["affine"]
    with ExitStack() as ctx:
        def sb(name, shape, dt=F32):
            return ctx.enter_context(nc.sbuf_tensor("node_" + name, shape, dt))

        def ps(name, shape):
            return ctx.enter_context(nc.psum_tensor("node_" + name, shape, F32))

        def sem(name):
            return ctx.enter_context(nc.semaphore("node_" + name))

        o = sb("o", [P, J, sz.half])
        squares = sb("squares", [P, 3, sz.half])
        rows = [sb(f"rows{s}", [P, J, 2, C]) for s in range(2)]
        msg_t = [sb(f"msg_t{s}", [P, J, P]) for s in range(2)]
        a = [sb(f"a{s}", [P, J, P]) for s in range(2)]
        a_sq = [sb(f"a_sq{s}", [P, 3, P]) for s in range(2)]
        b = [sb(f"b{s}", [P, J, P]) for s in range(2)]
        vv = [sb(f"vv{s}", [P, P]) for s in range(2)]
        acc0 = sb("acc0", [P, P])
        acc1 = sb("acc1", [P, P])
        tr_ps = [ps(f"tr_ps{s}", [P, J, P]) for s in range(2)]
        a_ps = [ps(f"a_ps{s}", [P, J, P]) for s in range(2)]
        o_ps = [ps(f"o_ps{s}", [P, J, P]) for s in range(2)]
        stat_ps = ps("stat_ps", [P, 3])
        total = sb("total", [P, 3])
        mean = sb("mean", [P, 2])
        power = sb("power", [P, 2])
        root = sb("root", [P, 2])
        gain = sb("gain", [P, 4])
        shift = sb("shift", [P, 2])
        z = [sb(f"z{s}", [P, J, P]) for s in range(2)]
        bn = [sb(f"bn{s}", [P, 2, 6]) for s in range(2)]
        mv = [sb(f"mv{s}", [P, 2, 2]) for s in range(2)]
        sd = [sb(f"sd{s}", [P, 2]) for s in range(2)]
        rs = [sb(f"rs{s}", [P, 2]) for s in range(2)]
        nb = [sb(f"nb{s}", [P, 2]) for s in range(2)]
        y = [sb(f"y{s}", [P, 2, F]) for s in range(2)]

        rows_in = [sem(f"rows_in{s}") for s in range(2)]
        turned, turned_out = sem("turned"), sem("turned_out")
        a_done, a_out = sem("a_done"), sem("a_out")
        vv_done, poly_step, b_done = sem("vv_done"), sem("poly_step"), sem("b_done")
        o_done, o_out = sem("o_done"), sem("o_out")
        total0, mean_done, totals12 = sem("total0"), sem("mean_done"), sem("totals12")
        folded, power_done, root_done = sem("folded"), sem("power_done"), sem("root_done")
        gain_step = sem("gain_step")
        z_done, z_turned = sem("z_done"), sem("z_turned")
        bn_step, mv_done, sd_done = sem("bn_step"), sem("mv_done"), sem("sd_done")
        rs_done, nb_done = sem("rs_done"), sem("nb_done")
        moments_cleared = sem("moments_cleared")
        y_done = sem("y_done")
        y_out = [sem(f"y_out{s}") for s in range(2)]

        def features(row, bank, h):
            cols = slice(h * C, (h + 1) * C)
            return ((row[:, 0:C], bank[:, 0, cols]),
                    (row[:, C:F].rearrange("p (c k) -> p k c", k=3), bank[:, 1:4, cols]))

        block = ctx.enter_context(nc.Block())

        @block.sync
        def _(sp):
            def load(i, s):
                n = 2 * i + s
                at_least(sp, turned, n - 1)
                for h in range(2):
                    sp.dma_start(rows[s][:, :, h, :],
                                 sums_dram[bass.ds(n * P + h * sz.half, P), :].rearrange("p (j c) -> p j c", j=J)).then_inc(rows_in[s], 16)

            load(0, 0)
            load(0, 1)
            for n in (2, 3):
                load(n // 2, n % 2)
            with sp.Fori(2, N // 2) as i:
                for s in range(2):
                    load(i, s)

            def store(i, s):
                n = 2 * i + s
                sp.wait_ge(y_done, n + 1)
                for h in range(2):
                    sp.dma_start(out[bass.ds(n * P + h * sz.half, P), :],
                                 y[s][:, h, :]).then_inc(y_out[s], 16)

            with sp.Fori(0, N // 2) as i:
                for s in range(2):
                    store(i, s)
            for s in range(2):
                sp.wait_ge(y_out[s], 32 * (N // 2))

        @block.tensor
        def _(pe):
            def turn(i, s):
                n = 2 * i + s
                pe.wait_ge(rows_in[s], 32 * (i + 1))
                at_least(pe, turned_out, n - 1)
                for j in range(J):
                    last = nc.tensor.transpose(tr_ps[s][:, j, :], rows[s][:, j, :, :], identity[:, :])
                last.then_inc(turned, 1)

            def linear(n, s):
                pe.wait_ge(turned_out, n + 1)
                at_least(pe, a_out, 2 * (n - 1))
                nc.tensor.matmul(a_ps[s][:, 0, :], w_lin[:, 0, :], msg_t[s][:, 0, :], start=True, stop=True)
                nc.tensor.matmul(a_ps[s][:, 1:4, :], w_lin[:, 1, :], msg_t[s][:, 1:4, :],
                                 start=True, stop=True).then_inc(a_done, 1)

            def back(n, s):
                at_least(pe, o_out, n - 1)
                here = x[:, :, bass.ds(n * P, P)]
                nc.tensor.matmul(o_ps[s][:, 0, :], w_self[:, 0, :], here[:, 0, :], start=True, stop=False)
                pe.wait_ge(b_done, 2 * n + 2)
                nc.tensor.matmul(o_ps[s][:, 0, :], w_back[:, 0, :], b[s][:, 0, :], start=False, stop=True)
                nc.tensor.matmul(o_ps[s][:, 1:4, :], w_self[:, 1, :], here[:, 1:4, :], start=True, stop=False)
                nc.tensor.matmul(o_ps[s][:, 1:4, :], w_back[:, 1, :], b[s][:, 1:4, :],
                                 start=False, stop=True).then_inc(o_done, 1)

            def forward(i, s):
                n = 2 * i + s
                static = isinstance(n, int)
                if not (static and n + 2 >= N):
                    turn(i + 1, s)
                if not (static and n + 1 >= N):
                    linear(n + 1, 1 - s)
                back(n, s)

            turn(0, 0)
            turn(0, 1)
            linear(0, 0)
            in_pairs(pe, forward, N)

            pe.wait_ge(total0, 1)
            nc.tensor.matmul(stat_ps[:, 0:1], fold_halves[:, :], total[:, 0:1], start=True, stop=True).then_inc(folded, 1)
            pe.wait_ge(totals12, 3)
            pe.wait_ge(mean_done, 1)
            nc.tensor.matmul(stat_ps[:, 1:3], fold_halves[:, :], total[:, 1:3], start=True, stop=True).then_inc(folded, 1)

            def turn_back(i, s):
                n = 2 * i + s
                pe.wait_ge(z_done, 2 * n + 2)
                at_least(pe, y_done, n - 1)
                for j in range(J):
                    last = nc.tensor.transpose(tr_ps[s][:, j, :], z[s][:, j, :], identity[:, :])
                last.then_inc(z_turned, 1)

            in_pairs(pe, turn_back, N)

        @block.scalar
        def _(act):
            def turn_copy(n, s):
                act.wait_ge(turned, n + 1)
                at_least(act, a_done, n - 1)
                nc.scalar.activation(msg_t[s][:, :, :], tr_ps[s][:, :, :], ACT.Copy).then_inc(turned_out, 1)

            def a_copy(n, s):
                act.wait_ge(a_done, n + 1)
                at_least(act, b_done, 2 * (n - 1))
                nc.scalar.activation(a[s][:, :, :], a_ps[s][:, :, :], ACT.Copy).then_inc(a_out, 1)
                nc.scalar.activation(a_sq[s][:, :, :], a_ps[s][:, 1:4, :], ACT.Square).then_inc(a_out, 1)

            def forward(i, s):
                n = 2 * i + s
                static = isinstance(n, int)
                if not (static and n + 2 >= N):
                    turn_copy(n + 2, s)
                if not (static and n + 1 >= N):
                    a_copy(n + 1, 1 - s)
                act.wait_ge(o_done, n + 1)
                nc.scalar.activation(o[:, :, bass.ds(n * P, P)], o_ps[s][:, :, :], ACT.Copy).then_inc(o_out, 1)

            turn_copy(0, 0)
            turn_copy(1, 1)
            a_copy(0, 0)
            in_pairs(act, forward, N)

            act.wait_ge(o_out, N)
            nc.scalar.activation(squares[:, :, :], o[:, 1:4, :], ACT.Square,
                                 accum_out=total[:, 2:3]).then_inc(totals12, 1)
            act.wait_ge(mean_done, 1)
            act.wait_ge(totals12, 1)
            for h, real in enumerate((sz.half, sz.second)):
                part = slice(h * C, (h + 1) * C)
                nc.scalar.activation(squares[part, 0, 0:real], o[part, 0, 0:real], ACT.Square,
                                     bias=mean[part, 1:2], accum_out=total[part, 1:2]).then_inc(totals12, 1)
            act.wait_ge(power_done, 2)
            nc.scalar.activation(root[:, :], power[:, :], ACT.Sqrt, bias=eps_col[:, 0:1]).then_inc(root_done, 1)

            def finish(i, s):
                n = 2 * i + s
                act.wait_ge(mv_done, 2 * n + 2)
                nc.scalar.activation(sd[s][:, :], mv[s][:, :, 1], ACT.Sqrt, bias=eps_col[:, 0:1]).then_inc(sd_done, 1)
                act.wait_ge(nb_done, n + 1)
                at_least(act, y_out[s], 32 * i)
                for h in range(2):
                    for to, frm in features(y[s][:, h, :], tr_ps[s], h):
                        last = nc.scalar.activation(to, frm, ACT.Identity, bias=nb[s][:, h:h + 1],
                                                    scale=rs[s][:, h:h + 1])
                last.then_inc(y_done, 1)

            in_pairs(act, finish, N)

        @block.vector
        def _(dve):
            def contract(i, s):
                n = 2 * i + s
                a0 = a[s][:, 0, :]
                dve.wait_ge(a_out, 2 * n + 2)
                at_least(dve, o_done, n - 1)
                nc.vector.tensor_tensor(vv[s][:, :], a_sq[s][:, 0, :], a_sq[s][:, 1, :], ALU.add).then_inc(vv_done, 1)
                nc.vector.tensor_scalar(acc0[:, :], a0, poly0[:, 3:4], poly0[:, 1:2], ALU.mult, ALU.add)
                nc.vector.tensor_scalar(acc1[:, :], a0, poly1[:, 2:3], poly1[:, 1:2], ALU.mult, ALU.add).then_inc(poly_step, 1)
                dve.wait_ge(vv_done, 2 * n + 1)
                nc.vector.tensor_tensor(vv[s][:, :], vv[s][:, :], a_sq[s][:, 2, :], ALU.add).then_inc(vv_done, 1)
                dve.wait_ge(poly_step, 4 * n + 1)
                nc.vector.tensor_tensor(acc0[:, :], acc0[:, :], a0, ALU.mult)
                nc.vector.tensor_tensor(acc1[:, :], acc1[:, :], a0, ALU.mult).then_inc(poly_step, 1)
                dve.wait_ge(poly_step, 4 * n + 2)
                dve.wait_ge(vv_done, 2 * n + 2)
                nc.vector.scalar_tensor_tensor(out=acc0[:, :], in0=vv[s][:, :], scalar=poly0[:, 4:5], in1=acc0[:, :],
                                               op0=ALU.mult, op1=ALU.add)
                nc.vector.scalar_tensor_tensor(out=acc1[:, :], in0=vv[s][:, :], scalar=poly1[:, 3:4], in1=acc1[:, :],
                                               op0=ALU.mult, op1=ALU.add).then_inc(poly_step, 1)
                dve.wait_ge(poly_step, 4 * n + 3)
                nc.vector.scalar_tensor_tensor(out=acc0[:, :], in0=acc0[:, :], scalar=poly0[:, 0:1], in1=a0,
                                               op0=ALU.add, op1=ALU.mult).then_inc(poly_step, 1)
                nc.vector.scalar_tensor_tensor(out=b[s][:, 1:4, :],
                                               in0=acc1[:, :].unsqueeze(1).to_broadcast([P, 3, P]),
                                               scalar=poly1[:, 0:1], in1=a[s][:, 1:4, :],
                                               op0=ALU.add, op1=ALU.mult).then_inc(b_done, 1)
                dve.wait_ge(poly_step, 4 * n + 4)
                nc.vector.scalar_tensor_tensor(out=b[s][:, 0, :], in0=vv[s][:, :], scalar=poly0[:, 2:3], in1=acc0[:, :],
                                               op0=ALU.mult, op1=ALU.add).then_inc(b_done, 1)
                dve.wait_ge(b_done, 2 * n + 2)

            in_pairs(dve, contract, N)

            nodes = float(sz.nodes)
            dve.wait_ge(o_out, N)
            nc.vector.tensor_reduce(total[:, 0:1], o[:, 0, :], AX.X, ALU.add).then_inc(total0, 1)
            dve.wait_ge(folded, 1)
            nc.vector.tensor_scalar(mean[:, 0:1], stat_ps[:, 0:1], 1.0 / nodes, None, ALU.mult)
            nc.vector.tensor_scalar(mean[:, 1:2], stat_ps[:, 0:1], -1.0 / nodes, None, ALU.mult).then_inc(mean_done, 1)
            dve.wait_ge(folded, 2)
            nc.vector.tensor_scalar(power[:, 0:1], stat_ps[:, 1:2], 1.0 / nodes, None, ALU.mult).then_inc(power_done, 1)
            nc.vector.tensor_scalar(power[:, 1:2], stat_ps[:, 2:3], 1.0 / (3 * nodes), None, ALU.mult).then_inc(power_done, 1)
            dve.wait_ge(root_done, 1)
            nc.vector.reciprocal(gain[:, 0:2], root[:, :]).then_inc(gain_step, 1)
            dve.wait_ge(gain_step, 1)
            nc.vector.tensor_tensor(gain[:, 2:3], gain[:, 0:1], affine[:, 0:1], ALU.mult)
            nc.vector.tensor_tensor(gain[:, 3:4], gain[:, 1:2], affine[:, 2:3], ALU.mult).then_inc(gain_step, 1)
            dve.wait_ge(gain_step, 2)
            nc.vector.tensor_tensor(shift[:, 0:1], mean[:, 1:2], gain[:, 2:3], ALU.mult).then_inc(gain_step, 1)
            dve.wait_ge(gain_step, 3)
            nc.vector.tensor_tensor(shift[:, 1:2], shift[:, 0:1], affine[:, 1:2], ALU.add).then_inc(gain_step, 1)
            dve.wait_ge(gain_step, 4)
            nc.vector.tensor_scalar(x[:, 0, :], x[:, 0, :], shift[:, 1:2], None, ALU.add).then_inc(gain_step, 1)
            dve.wait_ge(gain_step, 5)

            def residual(n, s):
                at_least(dve, z_turned, n - 1)
                at = bass.ds(n * P, P)
                for j, k, g in ((0, 1, 2), (1, 4, 3)):
                    nc.vector.scalar_tensor_tensor(out=z[s][:, j:k, :], in0=o[:, j:k, at], scalar=gain[:, g:g + 1],
                                                   in1=x[:, j:k, at], op0=ALU.mult, op1=ALU.add).then_inc(z_done, 1)

            def moments(n, s):
                dve.wait_ge(z_turned, n + 1)
                at_least(dve, sd_done, n - 1)
                for h in range(2):
                    nc.vector.bn_stats(bn[s][:, h, :], tr_ps[s][:, :, h * C:(h + 1) * C]).then_inc(bn_step, 1)
                for h in range(2):
                    dve.wait_ge(bn_step, 2 * n + h + 1)
                    clear(dve, moments_cleared)
                    nc.vector.bn_aggr(mv[s][:, h, :], bn[s][:, h, :]).then_inc(mv_done, 1)

            def finish(n, s):
                dve.wait_ge(sd_done, n + 1)
                at_least(dve, y_done, n - 1)
                nc.vector.reciprocal(rs[s][:, :], sd[s][:, :]).then_inc(rs_done, 1)
                dve.wait_ge(rs_done, n + 1)
                nc.vector.scalar_tensor_tensor(out=nb[s][:, :], in0=mv[s][:, :, 0], scalar=-1.0, in1=rs[s][:, :],
                                               op0=ALU.mult, op1=ALU.mult).then_inc(nb_done, 1)

            def step(i, s):
                n = 2 * i + s
                static = isinstance(n, int)
                residual(n, s)
                if not (static and n < 1):
                    moments(n - 1, 1 - s)
                    finish(n - 1, 1 - s)

            in_pairs(dve, step, N)
            dve.wait_ge(z_turned, N)
            moments(N - 1, 1)
            finish(N - 1, 1)


def lay_out_weights(w):
    import numpy as np

    def two_blocks(m):
        both = np.zeros((2 * m.shape[0], 2 * m.shape[1]), m.dtype)
        both[:m.shape[0], :m.shape[1]] = m
        both[m.shape[0]:, m.shape[1]:] = m
        return both

    def scalar_vector(name):
        return np.concatenate([two_blocks(w[name + "0"]), two_blocks(w[name + "1"])], axis=1)

    m4 = np.concatenate([w["M4"][:, part * C:(part + 1) * C] for part in (0, 2, 3, 1)], axis=1)
    affine = np.stack([w["gamma0"], w["beta0"], w["gamma1"]], axis=1)
    parts = {
        "w_lin": scalar_vector("W_lin"), "w_self": scalar_vector("Wsc"), "w_back": scalar_vector("WB"),
        "w_m1": np.pad(two_blocks(w["M1"]), ((0, P - 2 * w["M1"].shape[0]), (0, 0))),
        "w_m2": two_blocks(w["M2"]), "w_m3": two_blocks(w["M3"]), "w_m4": two_blocks(m4),
        "poly0": np.tile(w["Wc0"], (2, 1)), "poly1": np.tile(w["Wc1"], (2, 1)), "affine": np.tile(affine, (2, 1)),
    }
    return scalar_vector("W_up"), np.concatenate([parts[name] for name, _width in WEIGHT_PARTS], axis=1)


def kernel(x, src, dst, edge_attr_16, edge_attr_4, **layer):
    import numpy as np
    import concourse.bacc as bacc
    from concourse.bass_utils import run_bass_kernel_spmd as run

    x, src, dst, rbf, sh = (np.asarray(v) for v in (x, src, dst, edge_attr_16, edge_attr_4))
    sz = Shapes(x.shape[0], src.shape[0])
    more = sz.padded_edges - sz.edges
    xp = np.pad(x, ((0, sz.rows - sz.nodes), (0, 0)))
    comps = np.concatenate([xp[:, None, :C], xp[:, C:].reshape(sz.rows, C, 3).transpose(0, 2, 1)], axis=1)
    x_cm = comps.reshape(2, sz.half, J, C).transpose(0, 3, 2, 1).reshape(P, J, sz.half)
    src_p = np.pad(src, (0, more), mode="edge").reshape(sz.groups, TG, P)
    dst_p = np.pad(dst, (0, more), mode="edge").reshape(sz.groups, TG, P)
    sh_p = np.pad(sh, ((0, more), (0, 0))).reshape(sz.groups, TG, P, 4)
    rbf_p = np.pad(rbf, ((0, more), (0, 0))).reshape(sz.groups, 2, 4 * P, 16)
    arrays = {
        "x_cm": x_cm,
        "src_idx": src_p.transpose(0, 2, 1).reshape(sz.groups * P, TG),
        "dst_pt": dst_p.transpose(2, 0, 1).reshape(P, sz.tiles),
        "dst_rows": dst_p.reshape(sz.groups, GE),
        "first_dst": dst_p[:, 0, 0].reshape(1, sz.groups),
        "sh_in": sh_p.transpose(0, 2, 1, 3).reshape(sz.groups * P, TG * 4),
        "rbf_in": rbf_p.transpose(0, 1, 3, 2).reshape(sz.groups * 32, 4 * P),
    }
    arrays["w_up"], arrays["table"] = lay_out_weights(
        {name.removeprefix("L0_gnn_"): np.asarray(v) for name, v in layer.items()})
    arrays = {name: np.ascontiguousarray(a) for name, a in arrays.items()}
    nc = bacc.Bacc("TRN2", target_bir_lowering=False, num_devices=1)
    aps = {name: nc.dram_tensor(name + "_dram", a.shape, mybir.dt.from_np(a.dtype), kind="ExternalInput").ap()
           for name, a in arrays.items()}
    out = nc.dram_tensor("out_dram", (sz.rows, F), F32, kind="ExternalOutput").ap()
    build(nc, aps["x_cm"], aps["src_idx"], aps["dst_pt"], aps["dst_rows"], aps["first_dst"], aps["sh_in"],
          aps["rbf_in"], aps["w_up"], aps["table"], out, sz)
    result = run(nc, [{name + "_dram": a for name, a in arrays.items()}], core_ids=[0])
    return result.results[0]["out_dram"][:sz.nodes]
```

```python
from contextlib import ExitStack

import concourse.bass as bass
from concourse import mybir
from concourse.alu_op_type import AluOpType as ALU

ACT = mybir.ActivationFunctionType
AX = mybir.AxisListType
F32 = mybir.dt.float32
I32 = mybir.dt.int32
BF16 = mybir.dt.bfloat16

P = 128
C = 64
J = 4
F = J * C
TG = 8
GE = TG * P
SLOTS = 4
OWN_DOTS = 2
WINDOW = 80
EPS = 1e-5


WEIGHT_PARTS = (("w_lin", 2 * P), ("w_self", 2 * P), ("w_back", 2 * P), ("w_m1", P), ("w_m2", P), ("w_m3", P),
                ("w_m4", 2 * F), ("poly0", 5), ("poly1", 4), ("affine", 3))
WEIGHT_COLUMNS = sum(width for _name, width in WEIGHT_PARTS)


class Shapes:

    def __init__(self, nodes, edges):
        self.nodes = nodes
        self.edges = edges
        self.pairs = 2 * (-(-nodes // (4 * P)))
        self.half = self.pairs * P
        self.rows = 2 * self.half
        self.second = nodes - self.half
        self.groups = SLOTS * (-(-edges // (GE * SLOTS)))
        self.tiles = self.groups * TG
        self.padded_edges = self.groups * GE
        self.dump = self.rows
        self.sum_rows = self.rows + P


def at_least(engine, semaphore, value):
    if isinstance(value, int) and value <= 0:
        return
    engine.wait_ge(semaphore, value)


def clear(engine, passed):
    engine.sem_inc(passed, 1)


def run_steps(engine, step, steps, extra):
    first = 2 * SLOTS
    last = steps - SLOTS
    for g in range(min(first, steps)):
        step(g // SLOTS, g % SLOTS)
    if last > first:
        with engine.Fori(first // SLOTS, last // SLOTS) as i:
            for u in range(SLOTS):
                step(i, u)
    for g in range(max(last, first), steps + extra):
        step(g // SLOTS, g % SLOTS)


def in_pairs(engine, step, count, begin=0):
    last = count // 2 - 2
    for n in range(begin, min(4, count)):
        step(n // 2, n % 2)
    if last > 2:
        with engine.Fori(2, last) as i:
            for s in range(2):
                step(i, s)
    for n in range(max(4, 2 * last), count):
        step(n // 2, n % 2)


def slot_of(i, u, ahead=0):
    return i + (u + ahead) // SLOTS, (u + ahead) % SLOTS


def build(nc, x_cm, src_idx, dst_pt, dst_rows, first_dst, sh_in, rbf_in, w_up_dram, table_dram, out, sz):
    G = sz.groups
    with ExitStack() as top:
        def sem(name):
            return top.enter_context(nc.semaphore(name))

        def keep(name, shape, dt=F32):
            return top.enter_context(nc.sbuf_tensor(name, shape, dt))

        up_dram = nc.dram_tensor("up_rows", (sz.rows, F), F32, kind="Internal").ap()
        sums_dram = nc.dram_tensor("message_sums", (sz.sum_rows, F), F32, kind="Internal").ap()

        identity = keep("identity", [P, P])
        fold_halves = keep("fold_halves", [P, P])
        x = keep("x", [P, J, sz.half])
        w_up = keep("w_up", [P, 2, P])
        table = keep("table", [P, WEIGHT_COLUMNS])
        at = 0
        parts = {}
        for name, width in WEIGHT_PARTS:
            parts[name] = table[:, at:at + width]
            at += width
        w_m4 = parts["w_m4"]
        zeros = keep("zeros", [P, F])
        eps_col = keep("eps_col", [P, 1])
        lane_row = keep("lane_row", [P, P])
        lane_col = keep("lane_col", [P, 1])
        rel = keep("rel", [P, sz.tiles])
        base_f = keep("base_f", [P, G])
        window_rows = keep("window_rows", [P, G], I32)
        lower = keep("lower", [P, P])
        misfit = keep("misfit", [1, 1], I32)
        idx = [keep(f"idx{s}", [P, TG], I32) for s in range(SLOTS)]
        sh = [keep(f"sh{s}", [P, TG, 4]) for s in range(SLOTS)]
        rbf = [keep(f"rbf{s}", [32, 4 * P]) for s in range(SLOTS)]
        loaded = [sem(f"loaded{s}") for s in range(SLOTS)]
        table_in = sem("table_in")
        zeroed = sem("zeroed")

        def load_edges(sp, g, u):
            sp.dma_start(idx[u][:, :], src_idx[bass.ds(g * P, P), :]).then_inc(loaded[u], 16)
            sp.dma_start(rbf[u][:, :], rbf_in[bass.ds(g * 32, 32), :]).then_inc(loaded[u], 16)
            sp.dma_start(sh[u][:, :, :].rearrange("p t k -> p (t k)"),
                         sh_in[bass.ds(g * P, P), :]).then_inc(loaded[u], 16)

        with ExitStack() as ctx:
            def sb(name, shape, dt=F32):
                return ctx.enter_context(nc.sbuf_tensor(name, shape, dt))

            CH = 2
            chunks = sz.pairs // CH
            lane_row_i = sb("lane_row_i", [P, P], I32)
            lane_col_i = sb("lane_col_i", [P, 1], I32)
            ones = sb("ones", [P, P])
            dst_i = sb("dst_i", [P, sz.tiles], I32)
            base_i = sb("base_i", [P, G], I32)
            x_ring = [sb(f"x_ring{s}", [P, J, CH * P]) for s in range(2)]
            rows_f = sb("rows_f", [P, G])
            far = sb("far", [P, 4])
            up_sb = [sb(f"up_sb{s}", [P, CH, 2, J, C]) for s in range(2)]
            up_ps = [[ctx.enter_context(nc.psum_tensor(f"up_ps{s}_{q}", [P, J, 2, C], F32))
                      for q in range(CH)] for s in range(2)]
            count_ps = ctx.enter_context(nc.psum_tensor("count_ps", [P, 1], F32))

            w_up_in = sem("p1_w_up_in")
            dst_in = sem("p1_dst_in")
            x_in = [sem(f"p1_x_in{s}") for s in range(2)]
            up_done = sem("p1_up_done")
            x_kept = sem("p1_x_kept")
            copied = sem("p1_copied")
            up_out = [sem(f"p1_up_out{s}") for s in range(2)]
            patterns = sem("p1_patterns")
            dve_step = sem("p1_dve_step")
            far_made = sem("p1_far_made")
            counted = sem("p1_counted")

            block = ctx.enter_context(nc.Block())

            @block.sync
            def _(sp):
                sp.dma_start(w_up[:, :, :].rearrange("p v c -> p (v c)"), w_up_dram).then_inc(w_up_in, 16)

                def load(i, s):
                    k = 2 * i + s
                    at_least(sp, up_done, CH * (k - 1))
                    at_least(sp, x_kept, k - 1)
                    sp.dma_start(x_ring[s][:, :, :],
                                 x_cm[:, :, bass.ds(k * (CH * P), CH * P)]).then_inc(x_in[s], 16)

                load(0, 0)
                load(0, 1)
                sp.dma_start(dst_i[:, :], dst_pt).then_inc(dst_in, 16)
                sp.dma_start(base_i[:, :], first_dst.to_broadcast([P, G])).then_inc(dst_in, 16)
                sp.dma_start(table[:, :], table_dram).then_inc(table_in, 16)
                in_pairs(sp, load, chunks, 2)
                for g in range(SLOTS):
                    load_edges(sp, g, g)
                for s in range(2):
                    sp.wait_ge(up_out[s], 32 * ((chunks + 1 - s) // 2))

            @block.gpsimd
            def _(pool):
                nc.gpsimd.memset(identity[:, :], 0.0).then_inc(patterns, 1)
                nc.gpsimd.memset(lower[:, :], 1.0).then_inc(patterns, 1)
                nc.gpsimd.iota(lane_row_i[:, :], [[1, P]], base=0, channel_multiplier=0).then_inc(patterns, 1)
                nc.gpsimd.iota(lane_col_i[:, :], [[0, 1]], base=0, channel_multiplier=1).then_inc(patterns, 1)
                pool.wait_ge(patterns, 4)
                nc.gpsimd.affine_select(out=identity[:, :], in_=identity[:, :], compare_op=ALU.not_equal,
                                        fill=1.0, base=0, pattern=[[-1, P]],
                                        channel_multiplier=1).then_inc(patterns, 1)
                nc.gpsimd.affine_select(out=lower[:, :], in_=lower[:, :], compare_op=ALU.is_gt,
                                        fill=0.0, base=0, pattern=[[-1, P]],
                                        channel_multiplier=1).then_inc(patterns, 1)

            @block.scalar
            def _(act):
                def project(i, s):
                    k = 2 * i + s
                    at_least(act, up_out[s], 32 * i)
                    for q in range(CH):
                        act.wait_ge(up_done, CH * k + q + 1)
                        nc.scalar.activation(up_sb[s][:, q, :, :, :].rearrange("p h j c -> p j h c"),
                                             up_ps[s][q][:, :, :, :], ACT.Copy).then_inc(copied, 1)
                    act.wait_ge(copied, CH * (k + 1))
                    for h in range(2):
                        act.dma_start(
                            up_dram[bass.ds(k * (CH * P) + h * sz.half, CH * P), :]
                            .rearrange("(q p) f -> p q f", p=P),
                            up_sb[s][:, :, h, :, :].rearrange("p q j c -> p q (j c)"),
                        ).then_inc(up_out[s], 16)

                in_pairs(act, project, chunks)

            @block.vector
            def _(dve):
                nc.vector.memset(zeros[:, :], 0.0)
                nc.vector.memset(ones[:, :], 1.0)
                nc.vector.memset(eps_col[:, :], EPS).then_inc(dve_step, 1)

                def keep_nodes(i, s):
                    k = 2 * i + s
                    dve.wait_ge(x_in[s], 16 * (i + 1))
                    nc.vector.tensor_copy(x[:, :, bass.ds(k * (CH * P), CH * P)],
                                          x_ring[s][:, :, :]).then_inc(x_kept, 1)

                def patterns_and_fold():
                    dve.wait_ge(patterns, 6)
                    nc.vector.tensor_copy(lane_row[:, :], lane_row_i[:, :])
                    nc.vector.tensor_copy(lane_col[:, :], lane_col_i[:, :])
                    for h in range(2):
                        cols = slice(h * C, (h + 1) * C)
                        nc.vector.tensor_tensor(fold_halves[:, cols], identity[:, 0:C], identity[:, C:P], ALU.add)

                def relative_destinations():
                    dve.wait_ge(dst_in, 32)
                    nc.vector.tensor_copy(base_f[:, :], base_i[:, :]).then_inc(dve_step, 1)
                    nc.vector.tensor_tensor(rel[:, :].rearrange("p (g t) -> p g t", t=TG),
                                            dst_i[:, :].rearrange("p (g t) -> p g t", t=TG),
                                            base_i[:, :].unsqueeze(2).to_broadcast([P, G, TG]), ALU.subtract)
                    dve.wait_ge(dve_step, 2)
                    nc.vector.tensor_scalar(rows_f[:, :], base_f[:, :], lane_col[:, 0:1], None,
                                            ALU.add).then_inc(dve_step, 1)
                    dve.wait_ge(dve_step, 3)
                    nc.vector.tensor_copy(window_rows[:, :], rows_f[:, :])

                def find_misfits():
                    nc.vector.tensor_reduce(far[:, 0:1], rel[:, :], AX.X, ALU.max)
                    nc.vector.tensor_reduce(far[:, 1:2], rel[:, :], AX.X, ALU.min).then_inc(dve_step, 1)
                    dve.wait_ge(dve_step, 4)
                    nc.vector.tensor_scalar(far[:, 2:3], far[:, 0:1], float(WINDOW), None, ALU.is_ge)
                    nc.vector.tensor_scalar(far[:, 3:4], far[:, 1:2], 0.0, None, ALU.is_lt).then_inc(dve_step, 1)
                    dve.wait_ge(dve_step, 5)
                    nc.vector.tensor_tensor(far[:, 0:1], far[:, 2:3], far[:, 3:4], ALU.max).then_inc(far_made, 1)

                def scale_dot_weights():
                    dve.wait_ge(table_in, 16)
                    for h in range(2):
                        dots = w_m4[:, h * F + 2 * C:h * F + 3 * C]
                        nc.vector.tensor_scalar(dots, dots, float(3.0 ** -0.5), None, ALU.mult).then_inc(dve_step, 1)
                    dve.wait_ge(dve_step, 7)

                stages = (patterns_and_fold, relative_destinations, find_misfits, scale_dot_weights)
                for k, stage in enumerate(stages):
                    if k < chunks:
                        keep_nodes(k // 2, k % 2)
                    stage()
                in_pairs(dve, keep_nodes, chunks, len(stages))
                dve.wait_ge(x_kept, chunks)
                dve.wait_ge(counted, 1)
                nc.vector.tensor_copy(misfit[:, :], count_ps[0:1, :]).then_inc(dve_step, 1)
                dve.wait_ge(dve_step, 8)

            @block.tensor
            def _(pe):
                pe.wait_ge(w_up_in, 16)

                def project(i, s):
                    k = 2 * i + s
                    pe.wait_ge(x_in[s], 16 * (i + 1))
                    at_least(pe, copied, CH * (k - 1))
                    for q in range(CH):
                        for j in range(J):
                            last = nc.tensor.matmul(up_ps[s][q][:, j, :, :],
                                                    x_ring[s][:, j, q * P:(q + 1) * P],
                                                    w_up[:, min(j, 1), :], start=True, stop=True)
                        last.then_inc(up_done, 1)

                in_pairs(pe, project, chunks)
                pe.wait_ge(far_made, 1)
                nc.tensor.matmul(count_ps[:, :], ones[:, :], far[:, 0:1], start=True, stop=True).then_inc(counted, 1)

        for general in (False, True):
            edges(nc, sz, general, up_dram, sums_dram, dst_rows, load_edges, idx, sh, rbf, loaded,
                  parts, zeros, zeroed, lane_row, lane_col, lower, rel, base_f, window_rows, misfit)

        node_phase(nc, sz, x, sums_dram, out, identity, fold_halves, parts, eps_col)


def edges(nc, sz, general, up_dram, sums_dram, dst_rows, load_edges, idx, sh, rbf, loaded,
          parts, zeros, zeroed, lane_row, lane_col, lower, rel, base_f, window_rows, misfit):
    G = sz.groups
    tag = "any_" if general else "win_"
    reduce_lag = 2
    copy_lag = 2 if general else 3
    scatter_lag = 5 if general else 6
    rows_lag = SLOTS
    copies = 2 if general else 1
    per_group = TG if general else 1
    window = P if general else WINDOW
    w_m1, w_m2, w_m3, w_m4 = parts["w_m1"][0:32, :], parts["w_m2"], parts["w_m3"], parts["w_m4"]
    with ExitStack() as ctx:
        def sb(name, shape, dt=F32):
            return ctx.enter_context(nc.sbuf_tensor(tag + name, shape, dt))

        def ps(name, shape):
            return ctx.enter_context(nc.psum_tensor(tag + name, shape, F32))

        def sem(name):
            return ctx.enter_context(nc.semaphore(tag + name))

        X = [sb(f"X{s}", [P, TG, C + F]) for s in range(SLOTS)]
        hid1 = sb("hid1", [P, 4 * P])
        hid2 = sb("hid2", [P, 4 * P])
        hid3 = [sb(f"hid3_{s}", [P, 4 * P]) for s in range(2)]
        scaled = [sb(f"scaled{s}", [P, TG, 2, C]) for s in range(2)]
        dots = [sb(f"dots{s}", [P, TG, 3, C]) for s in range(2)]
        dot01 = sb("dot01", [P, TG, C])
        part = sb("part", [P, TG, 5, C])
        msg = [sb(f"msg{s}", [P, TG, J, C]) for s in range(2)]
        hot = [sb(f"hot{s}", [P, TG, window]) for s in range(2)]
        sums = [sb(f"sums{s}", [window, F]) for s in range(2)]
        sums_at = [sb(f"sums_at{s}", [window, 1], I32) for s in range(2 if general else SLOTS)]
        if general:
            drow_i = [sb(f"drow_i{s}", [P, TG * P], I32) for s in range(SLOTS)]
            drow_f = sb("drow_f", [P, TG, P])
            before = sb("before", [P, TG, P], BF16)
            dst = sb("dst", [P, TG])
            earlier = sb("earlier", [P, TG])
            spare = sb("spare", [P, TG])
            rows_i = [sb(f"rows_i{s}", [P, TG], I32) for s in range(2)]
        hid_ps = [ps(f"hid_ps{b}", [P, 4 * P]) for b in range(2)]
        tpw_ps = [ps(f"tpw_ps{b}", [P, 2, J, C]) for b in range(4)]
        sum_ps = [ps(f"sum_ps{b}", [window, F]) for b in range(2)]

        drow_in = [sem(f"drow_in{s}") for s in range(SLOTS)]
        gathered = [sem(f"gathered{s}") for s in range(SLOTS)]
        mm1, mm2, mm3 = sem("mm1"), sem("mm2"), sem("mm3")
        act1, act2, act3 = sem("act1"), sem("act2"), sem("act3")
        mm4 = sem("mm4")
        scaled_done = sem("scaled_done")
        own_dots_done = sem("own_dots_done")
        dots_done = sem("dots_done")
        dot01_done, u_done = sem("dot01_done"), sem("u_done")
        part_done = sem("part_done")
        hot_done = sem("hot_done")
        cross_done = sem("cross_done")
        own_done = sem("own_done")
        msg_done = sem("msg_done")
        summed = sem("summed")
        sums_out = sem("sums_out")
        rows_in = [sem(f"rows_in{s}") for s in range(SLOTS)]
        scattered = sem("scattered")
        gathers_cleared, scatters_cleared = sem("gathers_cleared"), sem("scatters_cleared")
        rank_step = sem("rank_step")

        block = ctx.enter_context(nc.Block())
        n_in = 3

        def chosen(engine):
            count = engine.value_load(misfit[0:1, 0:1], min_val=0, max_val=P)
            return engine.If(count > 0 if general else count < 1)

        @block.sync
        def _(sp):
            def step(i, u):
                g = SLOTS * i + u
                static = isinstance(g, int)
                if not (static and g >= G):
                    load(g, i, u)
                if static and g == SLOTS - 1:
                    for quarter in range(2):
                        sp.wait_ge(gathered[quarter], 16 * TG)
                        zero_sums(quarter)
                if static and SLOTS <= g < SLOTS + 2:
                    zero_sums(g - 2)
                if not general and not (static and not 0 <= g - rows_lag < G):
                    at_least(sp, scattered, 16 * (g - rows_lag - SLOTS + 1))
                    sp.dma_start(sums_at[u][:, :],
                                 window_rows[0:window, bass.ds(g - rows_lag, 1)]).then_inc(rows_in[u], 16)

            def zero_sums(quarter):
                per = sz.sum_rows // P
                first, end = quarter * per // 4, (quarter + 1) * per // 4
                sp.dma_start(sums_dram.rearrange("(p r) f -> p r f", p=P)[:, first:end, :],
                             zeros[:, :].unsqueeze(1).to_broadcast([P, end - first, F])).then_inc(zeroed, 16)

            def load(g, i, u):
                at_least(sp, msg_done, g - SLOTS + 1)
                if not (isinstance(g, int) and g < SLOTS):
                    load_edges(sp, g, u)
                if general:
                    sp.dma_start(drow_i[u][:, :],
                                 dst_rows[bass.ds(g, 1), :].to_broadcast([P, GE])).then_inc(drow_in[u], 16)

            with chosen(sp):
                run_steps(sp, step, G, rows_lag)
                sp.wait_ge(scattered, 16 * G * per_group)

        @block.gpsimd
        def _(pool):
            def step(i, u):
                g = SLOTS * i + u
                static = isinstance(g, int)
                if not (static and g >= G):
                    pool.wait_ge(loaded[u], 16 * n_in * (i + 1))
                    at_least(pool, msg_done, g - SLOTS + 1)
                    clear(pool, gathers_cleared)
                    for t in range(TG):
                        pool.indirect_dma_start(
                            out=X[u][:, t, C:C + F], out_offset=None, in_=up_dram[:, :],
                            in_offset=bass.IndirectOffsetOnAxis(ap=idx[u][:, t:t + 1], axis=0),
                        ).then_inc(gathered[u], 16)
                done = g - scatter_lag
                if static and not 0 <= done < G:
                    return
                before_i, before_u = slot_of(i, u, -scatter_lag)
                for t in range(per_group):
                    n = done * per_group + t
                    s = t % 2 if general else before_u % 2
                    at = sums_at[s if general else before_u]
                    pool.wait_ge(sums_out, copies * (n + 1))
                    if not general:
                        pool.wait_ge(rows_in[before_u], 16 * (before_i + 1))
                    if static and n == 0:
                        pool.wait_ge(zeroed, 16 * 4)
                    at_least(pool, scattered, 16 * n)
                    clear(pool, scatters_cleared)
                    pool.indirect_dma_start(
                        out=sums_dram[:, :],
                        out_offset=bass.IndirectOffsetOnAxis(ap=at[:, 0:1], axis=0),
                        in_=sums[s][:, :], in_offset=None, compute_op=ALU.add,
                    ).then_inc(scattered, 16)

            with chosen(pool):
                run_steps(pool, step, G, scatter_lag)

        @block.tensor
        def _(pe):
            def layer1(i, u):
                g = SLOTS * i + u
                pe.wait_ge(loaded[u], 16 * n_in * (i + 1))
                at_least(pe, act2, g)
                nc.tensor.matmul(hid_ps[u % 2][:, :], w_m1[:, :], rbf[u][:, :],
                                 start=True, stop=True).then_inc(mm1, 1)

            def layer2(i, u):
                pe.wait_ge(act1, SLOTS * i + u + 1)
                nc.tensor.matmul(hid_ps[(u + 1) % 2][:, :], w_m2[:, :], hid1[:, :],
                                 start=True, stop=True).then_inc(mm2, 1)

            def layer3(i, u):
                pe.wait_ge(act2, SLOTS * i + u + 1)
                nc.tensor.matmul(hid_ps[u % 2][:, :], w_m3[:, :], hid2[:, :],
                                 start=True, stop=True).then_inc(mm3, 1)

            def layer4(g, u, q):
                if q == 0:
                    pe.wait_ge(act3, g + 1)
                at_least(pe, part_done, 4 * g - 4 + q + 1)
                nc.tensor.matmul(tpw_ps[q][:, :, :, :], hid3[u % 2][:, q * P:(q + 1) * P],
                                 w_m4[:, :], start=True, stop=True).then_inc(mm4, 1)

            def reduce_group(g, u):
                pe.wait_ge(hot_done, g + 1)
                pe.wait_ge(msg_done, g + 1)
                if not general:
                    at_least(pe, sums_out, g - 1)
                for t in range(TG):
                    n = g * TG + t
                    if general:
                        at_least(pe, sums_out, 2 * (n - 1))
                    b = t % 2 if general else u % 2
                    done = nc.tensor.matmul(sum_ps[b][:, :], hot[u % 2][:, t, :],
                                            msg[u % 2][:, t, :, :],
                                            start=general or t == 0, stop=general or t == TG - 1)
                    if general:
                        done.then_inc(summed, 1)
                if not general:
                    done.then_inc(summed, 1)

            def step(i, u):
                g = SLOTS * i + u
                static = isinstance(g, int)
                ni, nu = slot_of(i, u, 1)
                ahead = not (static and g + 1 >= G)
                here = not (static and g >= G)
                if ahead:
                    layer1(ni, nu)
                if here:
                    layer4(g, u, 0)
                    layer4(g, u, 1)
                if ahead:
                    layer2(ni, nu)
                if here:
                    layer4(g, u, 2)
                    layer4(g, u, 3)
                if ahead:
                    layer3(ni, nu)
                if not (static and g < reduce_lag):
                    reduce_group(g - reduce_lag, (u - reduce_lag) % SLOTS)

            with chosen(pe):
                layer1(0, 0)
                layer2(0, 0)
                layer3(0, 0)
                run_steps(pe, step, G, reduce_lag)

        @block.scalar
        def _(act):
            def silu(layer, i, u):
                g = SLOTS * i + u
                ready = (mm1, mm2, mm3)[layer]
                out = (hid1, hid2, hid3[u % 2])[layer]
                bank = hid_ps[(u + layer % 2) % 2]
                act.wait_ge(ready, g + 1)
                nc.scalar.activation(out[:, :], bank[:, :], ACT.Silu).then_inc((act1, act2, act3)[layer], 1)

            def scale_weights(g, u, q):
                if q == 0:
                    at_least(act, own_done, 2 * (g - 1))
                act.wait_ge(mm4, 4 * g + q + 1)
                for h in range(2):
                    t = q + 4 * h
                    done = nc.scalar.activation(scaled[u % 2][:, t, :, :], tpw_ps[q][:, h, 0:2, :],
                                                ACT.Copy, scale=sh[u][:, t, 0:1])
                done.then_inc(scaled_done, 1)

            def dot_products(i, u, tiles):
                g = SLOTS * i + u
                if isinstance(g, int) and g < OWN_DOTS:
                    return
                if tiles[0] == 0:
                    act.wait_ge(loaded[u], 16 * n_in * (i + 1))
                    act.wait_ge(gathered[u], 16 * TG * (i + 1))
                    at_least(act, u_done, g - 1)
                for t in tiles:
                    for k in range(3):
                        done = nc.scalar.activation(dots[u % 2][:, t, k, :],
                                                    X[u][:, t, (2 + k) * C:(3 + k) * C],
                                                    ACT.Copy, scale=sh[u][:, t, k + 1:k + 2])
                if tiles[-1] == TG - 1:
                    done.then_inc(dots_done, 1)

            def copy_sums(g, u):
                for t in range(per_group):
                    n = g * per_group + t
                    b = t % 2 if general else u % 2
                    act.wait_ge(summed, n + 1)
                    at_least(act, scattered, 16 * (n - 1))
                    nc.scalar.activation(sums[b][:, :], sum_ps[b][:, :], ACT.Copy).then_inc(sums_out, 1)
                    if general:
                        nc.scalar.copy(sums_at[b][:, :], rows_i[u % 2][:, t:t + 1]).then_inc(sums_out, 1)

            def step(i, u):
                g = SLOTS * i + u
                static = isinstance(g, int)
                ni, nu = slot_of(i, u, 1)
                ahead = not (static and g + 1 >= G)
                here = not (static and g >= G)
                if static and g < 2:
                    silu(0, ni, nu)
                    scale_weights(g, u, 0)
                    scale_weights(g, u, 1)
                    silu(1, ni, nu)
                    scale_weights(g, u, 2)
                    scale_weights(g, u, 3)
                    silu(2, ni, nu)
                    dot_products(ni, nu, range(TG))
                    return
                if ahead:
                    silu(0, ni, nu)
                    dot_products(ni, nu, (0,))
                if here:
                    scale_weights(g, u, 0)
                    scale_weights(g, u, 1)
                if ahead:
                    dot_products(ni, nu, (1,))
                    silu(1, ni, nu)
                if here:
                    scale_weights(g, u, 2)
                if ahead:
                    dot_products(ni, nu, (2,))
                if here:
                    scale_weights(g, u, 3)
                if ahead:
                    silu(2, ni, nu)
                    dot_products(ni, nu, range(3, TG))
                if not (static and not 0 <= g - copy_lag < G):
                    copy_sums(g - copy_lag, (u - copy_lag) % SLOTS)

            with chosen(act):
                silu(0, 0, 0)
                silu(1, 0, 0)
                silu(2, 0, 0)
                run_steps(act, step, G, copy_lag)

        @block.vector
        def _(dve):
            def make_hot(g, i, u):
                if general:
                    dve.wait_ge(drow_in[u], 16 * (i + 1))
                at_least(dve, summed, per_group * (g - 1))
                here = rel[:, bass.ds(g * TG, TG)].unsqueeze(2).to_broadcast([P, TG, window])
                if general:
                    nc.vector.tensor_tensor(drow_f[:, :, :], drow_i[u][:, :].rearrange("p (t e) -> p t e", t=TG),
                                            base_f[:, bass.ds(g, 1)].unsqueeze(2).to_broadcast([P, TG, P]),
                                            ALU.subtract).then_inc(rank_step, 1)
                    dve.wait_ge(rank_step, 4 * g + 1)
                    lanes = drow_f[:, :, :]
                else:
                    lanes = lane_row[:, 0:window].unsqueeze(1).to_broadcast([P, TG, window])
                nc.vector.tensor_tensor(hot[u % 2][:, :, :], lanes, here, ALU.is_equal).then_inc(hot_done, 1)

            def rank(g, u):
                at_least(dve, sums_out, 2 * TG * (g - 1))
                dve.wait_ge(hot_done, g + 1)
                nc.vector.tensor_tensor(before[:, :, :], hot[u % 2][:, :, :],
                                        lower[:, :].unsqueeze(1).to_broadcast([P, TG, P]), ALU.mult)
                nc.vector.tensor_tensor(dst[:, :], rel[:, bass.ds(g * TG, TG)],
                                        base_f[:, bass.ds(g, 1)].to_broadcast([P, TG]),
                                        ALU.add).then_inc(rank_step, 1)
                dve.wait_ge(rank_step, 4 * g + 2)
                nc.vector.tensor_reduce(earlier[:, :], before[:, :, :], AX.X, ALU.max)
                nc.vector.tensor_scalar(spare[:, :], dst[:, :], -1.0,
                                        float(sz.dump), ALU.mult, ALU.add).then_inc(rank_step, 1)
                dve.wait_ge(rank_step, 4 * g + 3)
                nc.vector.tensor_scalar(earlier[:, :], earlier[:, :], 0.0, None, ALU.is_gt)
                nc.vector.tensor_scalar(spare[:, :], spare[:, :], lane_col[:, 0:1], None,
                                        ALU.add).then_inc(rank_step, 1)
                dve.wait_ge(rank_step, 4 * g + 4)
                nc.vector.tensor_tensor(spare[:, :], spare[:, :], earlier[:, :], ALU.mult).then_inc(cross_done, 1)
                dve.wait_ge(cross_done, 2 * g + 1)
                nc.vector.tensor_tensor(rows_i[u % 2][:, :], spare[:, :], dst[:, :], ALU.add)

            def sum_first(g, u):
                if isinstance(g, int) and g < OWN_DOTS:
                    dve.wait_ge(loaded[g], 16 * n_in)
                    dve.wait_ge(gathered[g], 16 * TG)
                    nc.vector.tensor_tensor(dots[u % 2][:, :, :, :],
                                            X[u][:, :, 2 * C:5 * C].rearrange("p t (k c) -> p t k c", k=3),
                                            sh[u][:, :, 1:4].unsqueeze(3).to_broadcast([P, TG, 3, C]),
                                            ALU.mult).then_inc(own_dots_done, 1)
                    dve.wait_ge(own_dots_done, g + 1)
                else:
                    dve.wait_ge(dots_done, g - OWN_DOTS + 1)
                nc.vector.tensor_tensor(dot01[:, :, :], dots[u % 2][:, :, 0, :], dots[u % 2][:, :, 1, :],
                                        ALU.add).then_inc(dot01_done, 1)

            def sum_last(g, u):
                dve.wait_ge(dot01_done, g + 1)
                nc.vector.tensor_tensor(X[u][:, :, 0:C], dot01[:, :, :], dots[u % 2][:, :, 2, :],
                                        ALU.add).then_inc(u_done, 1)

            def step(i, u):
                g = SLOTS * i + u
                static = isinstance(g, int)
                if static and g >= G:
                    return
                ahead = not (static and g + 1 >= G)
                nu = (u + 1) % SLOTS
                crosses = 2 * g + 2 if general else g + 1
                x = X[u]
                dve.wait_ge(u_done, g + 1)
                at_least(dve, msg_done, g)
                for q in range(4):
                    dve.wait_ge(scaled_done, 4 * g + q + 1)
                    nc.vector.tensor_tensor(
                        part[:, q::4, 0::4, :], tpw_ps[q][:, :, 2:4, :],
                        x[:, q::4, 0:2 * C].rearrange("p t (b c) -> p t b c", b=2), ALU.mult,
                    ).then_inc(part_done, 1)
                if general:
                    make_hot(g, i, u)
                    rank(g, u)
                at_least(dve, summed, per_group * (g - 1))
                nc.vector.tensor_tensor(msg[u % 2][:, :, 0, :], scaled[u % 2][:, :, 0, :],
                                        x[:, :, C:2 * C], ALU.mult).then_inc(own_done, 1)
                nc.vector.tensor_tensor(msg[u % 2][:, :, 1:4, :],
                                        scaled[u % 2][:, :, 1:2, :].to_broadcast([P, TG, 3, C]),
                                        x[:, :, 2 * C:5 * C].rearrange("p t (k c) -> p t k c", k=3),
                                        ALU.mult).then_inc(own_done, 1)
                dve.wait_ge(part_done, 4 * g + 4)
                nc.vector.tensor_tensor(part[:, :, 1:4, :], part[:, :, 4:5, :].to_broadcast([P, TG, 3, C]),
                                        sh[u][:, :, 1:4].unsqueeze(3).to_broadcast([P, TG, 3, C]),
                                        ALU.mult).then_inc(cross_done, 1)
                if ahead:
                    sum_first(g + 1, nu)
                dve.wait_ge(cross_done, crosses)
                dve.wait_ge(own_done, 2 * g + 2)
                nc.vector.tensor_tensor(msg[u % 2][:, :, :, :], msg[u % 2][:, :, :, :],
                                        part[:, :, 0:4, :], ALU.add).then_inc(msg_done, 1)
                if ahead:
                    sum_last(g + 1, nu)
                if not general:
                    make_hot(g, i, u)

            with chosen(dve):
                sum_first(0, 0)
                sum_last(0, 0)
                run_steps(dve, step, G, 0)


def node_phase(nc, sz, x, sums_dram, out, identity, fold_halves, parts, eps_col):
    N = sz.pairs
    Q = 2
    w_lin, w_self, w_back = (parts[name].rearrange("p (v c) -> p v c", v=2)
                             for name in ("w_lin", "w_self", "w_back"))
    poly0, poly1, affine = parts["poly0"], parts["poly1"], parts["affine"]
    with ExitStack() as ctx:
        def sb(name, shape, dt=F32):
            return ctx.enter_context(nc.sbuf_tensor("node_" + name, shape, dt))

        def ps(name, shape):
            return ctx.enter_context(nc.psum_tensor("node_" + name, shape, F32))

        def sem(name):
            return ctx.enter_context(nc.semaphore("node_" + name))

        o = sb("o", [P, J, sz.half])
        squares = sb("squares", [P, sz.half])
        step_squares = sb("step_squares", [P, N])
        rows = [sb(f"rows{s}", [P, J, 2, C]) for s in range(2)]
        msg_t = [sb(f"msg_t{s}", [P, J, P]) for s in range(2)]
        a = [sb(f"a{s}", [P, J, P]) for s in range(2)]
        a_sq = [sb(f"a_sq{s}", [P, 3, P]) for s in range(2)]
        b = [sb(f"b{s}", [P, J, P]) for s in range(2)]
        vv = [sb(f"vv{s}", [P, P]) for s in range(2)]
        acc0 = [sb(f"acc0{s}", [P, P]) for s in range(2)]
        acc1 = [sb(f"acc1{s}", [P, P]) for s in range(2)]
        unused = sb("unused", [P, 1])
        o0_sum = sb("o0_sum", [P, P])
        tr_ps = [ps(f"tr_ps{s}", [P, J, P]) for s in range(2)]
        a_ps = [ps(f"a_ps{s}", [P, J, P]) for s in range(2)]
        o_ps = [ps(f"o_ps{s}", [P, J, P]) for s in range(2)]
        stat_ps = ps("stat_ps", [P, 4])
        total = sb("total", [P, 4])
        mean = sb("mean", [P, 2])
        power = sb("power", [P, 2])
        root = sb("root", [P, 2])
        gain = sb("gain", [P, 4])
        shift = sb("shift", [P, 2])
        z = [sb(f"z{s}", [P, J, Q * P]) for s in range(2)]
        bn = [sb(f"bn{s}", [P, Q, 2, 6]) for s in range(2)]
        mv = [sb(f"mv{s}", [P, Q, 2, 2]) for s in range(2)]
        sd = [sb(f"sd{s}", [P, Q, 2]) for s in range(2)]
        rs = [sb(f"rs{s}", [P, Q, 2]) for s in range(2)]
        nb = [sb(f"nb{s}", [P, Q, 2]) for s in range(2)]
        y = [sb(f"y{s}", [P, Q, 2, F]) for s in range(2)]
        z_ps = [[tr_ps[s], o_ps[s]] for s in range(2)]

        rows_in = [sem(f"rows_in{s}") for s in range(2)]
        turned, turned_out = sem("turned"), sem("turned_out")
        a_done, a_out = sem("a_done"), sem("a_out")
        sq_done, vv_done, acc1_done = sem("sq_done"), sem("vv_done"), sem("acc1_done")
        poly_step, b_done = sem("poly_step"), sem("b_done")
        o0_step = sem("o0_step")
        o_done, o_out = sem("o_done"), sem("o_out")
        total0, mean_done, squares_done = sem("total0"), sem("mean_done"), sem("squares_done")
        total3, stat_step = sem("total3"), sem("stat_step")
        folded, power_done, root_done = sem("folded"), sem("power_done"), sem("root_done")
        gain_step = sem("gain_step")
        z_done, z_turned = sem("z_done"), sem("z_turned")
        bn_step, mv_done, sd_done = sem("bn_step"), sem("mv_done"), sem("sd_done")
        rs_done, nb_done = sem("rs_done"), sem("nb_done")
        moments_cleared = sem("moments_cleared")
        y_done = sem("y_done")
        y_out = [sem(f"y_out{s}") for s in range(2)]

        def features(row, bank, h):
            cols = slice(h * C, (h + 1) * C)
            return ((row[:, 0:C], bank[:, 0, cols]),
                    (row[:, C:F].rearrange("p (c k) -> p k c", k=3), bank[:, 1:4, cols]))

        block = ctx.enter_context(nc.Block())

        @block.sync
        def _(sp):
            def load(i, s):
                n = 2 * i + s
                at_least(sp, turned, n - 1)
                for h in range(2):
                    sp.dma_start(rows[s][:, :, h, :],
                                 sums_dram[bass.ds(n * P + h * sz.half, P), :].rearrange("p (j c) -> p j c", j=J)).then_inc(rows_in[s], 16)

            load(0, 0)
            load(0, 1)
            for n in (2, 3):
                load(n // 2, n % 2)
            with sp.Fori(2, N // 2) as i:
                for s in range(2):
                    load(i, s)

            def store(i, s):
                m = 2 * i + s
                sp.wait_ge(y_done, Q * (m + 1))
                for h in range(2):
                    sp.dma_start(out[bass.ds(m * (Q * P) + h * sz.half, Q * P), :].rearrange("(q p) f -> p q f", p=P),
                                 y[s][:, :, h, :]).then_inc(y_out[s], 16)

            in_pairs(sp, store, N // Q)
            for s in range(2):
                sp.wait_ge(y_out[s], 32 * ((N // Q + 1 - s) // 2))

        @block.gpsimd
        def _(pool):
            def squared_length(n, s):
                pool.wait_ge(sq_done, n + 1)
                at_least(pool, b_done, 2 * (n - 1))
                nc.gpsimd.tensor_tensor(vv[s][:, :], a_sq[s][:, 0, :], a_sq[s][:, 1, :], ALU.add).then_inc(vv_done, 1)
                pool.wait_ge(vv_done, 2 * n + 1)
                nc.gpsimd.tensor_tensor(vv[s][:, :], vv[s][:, :], a_sq[s][:, 2, :], ALU.add).then_inc(vv_done, 1)

            def forward(i, s):
                n = 2 * i + s
                if not (isinstance(n, int) and n + 2 >= N):
                    squared_length(n + 2, s)
                pool.wait_ge(o_out, n + 1)
                pool.wait_ge(o0_step, n + 1)
                nc.gpsimd.tensor_tensor(o0_sum[:, :], o0_sum[:, :], o[:, 0, bass.ds(n * P, P)],
                                        ALU.add).then_inc(o0_step, 1)

            nc.gpsimd.memset(o0_sum[:, :], 0.0).then_inc(o0_step, 1)
            squared_length(0, 0)
            squared_length(1, 1)
            in_pairs(pool, forward, N)

        @block.tensor
        def _(pe):
            def turn(i, s):
                n = 2 * i + s
                pe.wait_ge(rows_in[s], 32 * (i + 1))
                at_least(pe, turned_out, n - 1)
                for j in range(J):
                    last = nc.tensor.transpose(tr_ps[s][:, j, :], rows[s][:, j, :, :], identity[:, :])
                last.then_inc(turned, 1)

            def linear(n, s):
                pe.wait_ge(turned_out, n + 1)
                at_least(pe, a_out, 2 * (n - 1))
                nc.tensor.matmul(a_ps[s][:, 0, :], w_lin[:, 0, :], msg_t[s][:, 0, :], start=True, stop=True)
                nc.tensor.matmul(a_ps[s][:, 1:4, :], w_lin[:, 1, :], msg_t[s][:, 1:4, :],
                                 start=True, stop=True).then_inc(a_done, 1)

            def back(n, s):
                at_least(pe, squares_done, n - 1)
                here = x[:, :, bass.ds(n * P, P)]
                nc.tensor.matmul(o_ps[s][:, 0, :], w_self[:, 0, :], here[:, 0, :], start=True, stop=False)
                pe.wait_ge(b_done, 2 * n + 2)
                nc.tensor.matmul(o_ps[s][:, 0, :], w_back[:, 0, :], b[s][:, 0, :], start=False, stop=True)
                nc.tensor.matmul(o_ps[s][:, 1:4, :], w_self[:, 1, :], here[:, 1:4, :], start=True, stop=False)
                nc.tensor.matmul(o_ps[s][:, 1:4, :], w_back[:, 1, :], b[s][:, 1:4, :],
                                 start=False, stop=True).then_inc(o_done, 1)

            def forward(i, s):
                n = 2 * i + s
                static = isinstance(n, int)
                if not (static and n + 2 >= N):
                    linear(n + 2, s)
                if not (static and n + 3 >= N):
                    turn(i + 1 + s, 1 - s)
                back(n, s)

            turn(0, 0)
            turn(0, 1)
            linear(0, 0)
            turn(1, 0)
            linear(1, 1)
            in_pairs(pe, forward, N)

            pe.wait_ge(total0, 1)
            nc.tensor.matmul(stat_ps[:, 0:1], fold_halves[:, :], total[:, 0:1], start=True, stop=True).then_inc(folded, 1)
            pe.wait_ge(squares_done, N + 2)
            pe.wait_ge(total3, 1)
            pe.wait_ge(mean_done, 1)
            nc.tensor.matmul(stat_ps[:, 1:4], fold_halves[:, :], total[:, 1:4], start=True, stop=True).then_inc(folded, 1)

            def turn_back(i, s):
                m = 2 * i + s
                pe.wait_ge(z_done, 2 * m + 2)
                for q in range(Q):
                    at_least(pe, y_done, Q * (m - 2) + q + 1)
                    for j in range(J):
                        last = nc.tensor.transpose(z_ps[s][q][:, j, :], z[s][:, j, q * P:(q + 1) * P],
                                                   identity[:, :])
                    last.then_inc(z_turned, 1)

            in_pairs(pe, turn_back, N // Q)

        @block.scalar
        def _(act):
            def turn_copy(n, s):
                act.wait_ge(turned, n + 1)
                at_least(act, a_done, n - 1)
                nc.scalar.activation(msg_t[s][:, :, :], tr_ps[s][:, :, :], ACT.Copy).then_inc(turned_out, 1)

            def a_copy(n, s):
                act.wait_ge(a_done, n + 1)
                at_least(act, b_done, 2 * (n - 1))
                nc.scalar.activation(a_sq[s][:, :, :], a_ps[s][:, 1:4, :], ACT.Square).then_inc(sq_done, 1)
                nc.scalar.activation(acc1[s][:, :], a_ps[s][:, 0, :], ACT.Identity, bias=poly1[:, 1:2],
                                     scale=poly1[:, 2:3]).then_inc(a_out, 1)
                nc.scalar.activation(a[s][:, :, :], a_ps[s][:, :, :], ACT.Copy).then_inc(a_out, 1)

            def forward(i, s):
                n = 2 * i + s
                static = isinstance(n, int)
                if not (static and n + 2 >= N):
                    a_copy(n + 2, s)
                if not (static and n + 3 >= N):
                    turn_copy(n + 3, 1 - s)
                act.wait_ge(o_done, n + 1)
                nc.scalar.activation(o[:, :, bass.ds(n * P, P)], o_ps[s][:, :, :], ACT.Copy).then_inc(o_out, 1)
                at_least(act, squares_done, n)
                nc.scalar.activation(squares[:, 0:3 * P].rearrange("p (j c) -> p j c", j=3), o_ps[s][:, 1:4, :],
                                     ACT.Square, accum_out=step_squares[:, bass.ds(n, 1)]).then_inc(squares_done, 1)

            nc.scalar.activation(unused[:, :], eps_col[:, 0:1], ACT.Sqrt)
            turn_copy(0, 0)
            turn_copy(1, 1)
            a_copy(0, 0)
            turn_copy(2, 0)
            a_copy(1, 1)
            in_pairs(act, forward, N)

            act.wait_ge(o_out, N)
            act.wait_ge(squares_done, N)
            act.wait_ge(mean_done, 1)
            nc.scalar.activation(squares[:, 0:sz.second], o[:, 0, 0:sz.second], ACT.Square,
                                 bias=mean[:, 1:2], accum_out=total[:, 1:2]).then_inc(squares_done, 1)
            rest = slice(sz.second, sz.half)
            nc.scalar.activation(squares[0:C, rest], o[0:C, 0, rest], ACT.Square,
                                 bias=mean[0:C, 1:2], accum_out=total[0:C, 2:3]).then_inc(squares_done, 1)
            act.wait_ge(power_done, 2)
            nc.scalar.activation(root[:, :], power[:, :], ACT.Sqrt, bias=eps_col[:, 0:1]).then_inc(root_done, 1)

            def finish(i, s):
                m = 2 * i + s
                act.wait_ge(mv_done, 2 * Q * (m + 1))
                nc.scalar.activation(sd[s][:, :, :], mv[s][:, :, :, 1], ACT.Sqrt, bias=eps_col[:, 0:1]).then_inc(sd_done, 1)
                act.wait_ge(nb_done, m + 1)
                at_least(act, y_out[s], 32 * i)
                for q in range(Q):
                    for h in range(2):
                        for to, frm in features(y[s][:, q, h, :], z_ps[s][q], h):
                            last = nc.scalar.activation(to, frm, ACT.Identity, bias=nb[s][:, q, h:h + 1],
                                                        scale=rs[s][:, q, h:h + 1])
                    last.then_inc(y_done, 1)

            in_pairs(act, finish, N // Q)

        @block.vector
        def _(dve):
            def contract(i, s):
                n = 2 * i + s
                a0 = a[s][:, 0, :]
                acc0_s, acc1_s, vv_s = acc0[s][:, :], acc1[s][:, :], vv[s][:, :]
                dve.wait_ge(a_out, 2 * n + 2)
                nc.vector.tensor_scalar(acc0_s, a0, poly0[:, 3:4], poly0[:, 1:2], ALU.mult, ALU.add).then_inc(poly_step, 1)
                nc.vector.tensor_tensor(acc1_s, acc1_s, a0, ALU.mult).then_inc(poly_step, 1)
                dve.wait_ge(poly_step, 5 * n + 1)
                nc.vector.tensor_tensor(acc0_s, acc0_s, a0, ALU.mult).then_inc(poly_step, 1)
                dve.wait_ge(poly_step, 5 * n + 2)
                dve.wait_ge(vv_done, 2 * n + 2)
                nc.vector.scalar_tensor_tensor(out=acc1_s, in0=vv_s, scalar=poly1[:, 3:4], in1=acc1_s,
                                               op0=ALU.mult, op1=ALU.add).then_inc(acc1_done, 1)
                dve.wait_ge(poly_step, 5 * n + 3)
                nc.vector.scalar_tensor_tensor(out=acc0_s, in0=vv_s, scalar=poly0[:, 4:5], in1=acc0_s,
                                               op0=ALU.mult, op1=ALU.add).then_inc(poly_step, 1)
                dve.wait_ge(acc1_done, n + 1)
                at_least(dve, o_done, n - 1)
                nc.vector.scalar_tensor_tensor(out=b[s][:, 1:4, :],
                                               in0=acc1_s.unsqueeze(1).to_broadcast([P, 3, P]),
                                               scalar=poly1[:, 0:1], in1=a[s][:, 1:4, :],
                                               op0=ALU.add, op1=ALU.mult).then_inc(b_done, 1)
                dve.wait_ge(poly_step, 5 * n + 4)
                nc.vector.scalar_tensor_tensor(out=acc0_s, in0=acc0_s, scalar=poly0[:, 0:1], in1=a0,
                                               op0=ALU.add, op1=ALU.mult).then_inc(poly_step, 1)
                dve.wait_ge(poly_step, 5 * n + 5)
                nc.vector.scalar_tensor_tensor(out=b[s][:, 0, :], in0=vv_s, scalar=poly0[:, 2:3], in1=acc0_s,
                                               op0=ALU.mult, op1=ALU.add).then_inc(b_done, 1)

            in_pairs(dve, contract, N)

            nodes = float(sz.nodes)
            nc.vector.memset(total[C:P, 2:3], 0.0)
            dve.wait_ge(o0_step, N + 1)
            nc.vector.tensor_reduce(total[:, 0:1], o0_sum[:, :], AX.X, ALU.add).then_inc(total0, 1)
            dve.wait_ge(folded, 1)
            nc.vector.tensor_scalar(mean[:, 0:1], stat_ps[:, 0:1], 1.0 / nodes, None, ALU.mult)
            nc.vector.tensor_scalar(mean[:, 1:2], stat_ps[:, 0:1], -1.0 / nodes, None, ALU.mult).then_inc(mean_done, 1)
            dve.wait_ge(squares_done, N)
            nc.vector.tensor_reduce(total[:, 3:4], step_squares[:, :], AX.X, ALU.add).then_inc(total3, 1)
            dve.wait_ge(folded, 2)
            nc.vector.tensor_reduce(power[:, 0:1], stat_ps[:, 1:3], AX.X, ALU.add).then_inc(stat_step, 1)
            nc.vector.tensor_scalar(power[:, 1:2], stat_ps[:, 3:4], 1.0 / (3 * nodes), None, ALU.mult).then_inc(power_done, 1)
            dve.wait_ge(stat_step, 1)
            nc.vector.tensor_scalar(power[:, 0:1], power[:, 0:1], 1.0 / nodes, None, ALU.mult).then_inc(power_done, 1)
            dve.wait_ge(root_done, 1)
            nc.vector.reciprocal(gain[:, 0:2], root[:, :]).then_inc(gain_step, 1)
            dve.wait_ge(gain_step, 1)
            nc.vector.tensor_tensor(gain[:, 2:3], gain[:, 0:1], affine[:, 0:1], ALU.mult)
            nc.vector.tensor_tensor(gain[:, 3:4], gain[:, 1:2], affine[:, 2:3], ALU.mult).then_inc(gain_step, 1)
            dve.wait_ge(gain_step, 2)
            nc.vector.tensor_tensor(shift[:, 0:1], mean[:, 1:2], gain[:, 2:3], ALU.mult).then_inc(gain_step, 1)
            dve.wait_ge(gain_step, 3)
            nc.vector.tensor_tensor(shift[:, 1:2], shift[:, 0:1], affine[:, 1:2], ALU.add).then_inc(gain_step, 1)
            dve.wait_ge(gain_step, 4)
            nc.vector.tensor_scalar(x[:, 0, :], x[:, 0, :], shift[:, 1:2], None, ALU.add).then_inc(gain_step, 1)
            dve.wait_ge(gain_step, 5)

            def residual(m, s, parts):
                at_least(dve, z_turned, Q * (m - 1))
                at = bass.ds(m * (Q * P), Q * P)
                for j, k, g in parts:
                    nc.vector.scalar_tensor_tensor(out=z[s][:, j:k, :], in0=o[:, j:k, at], scalar=gain[:, g:g + 1],
                                                   in1=x[:, j:k, at], op0=ALU.mult, op1=ALU.add).then_inc(z_done, 1)

            scalar_part, vector_part = (0, 1, 2), (1, 4, 3)

            def moments(m, s):
                at_least(dve, sd_done, m - 1)
                for q in range(Q):
                    dve.wait_ge(z_turned, Q * m + q + 1)
                    for h in range(2):
                        nc.vector.bn_stats(bn[s][:, q, h, :],
                                           z_ps[s][q][:, :, h * C:(h + 1) * C]).then_inc(bn_step, 1)
                for q in range(Q):
                    for h in range(2):
                        dve.wait_ge(bn_step, 2 * Q * m + 2 * q + h + 1)
                        clear(dve, moments_cleared)
                        nc.vector.bn_aggr(mv[s][:, q, h, :], bn[s][:, q, h, :]).then_inc(mv_done, 1)

            def finish(m, s):
                dve.wait_ge(sd_done, m + 1)
                at_least(dve, y_done, Q * (m - 1))
                nc.vector.reciprocal(rs[s][:, :, :], sd[s][:, :, :]).then_inc(rs_done, 1)
                dve.wait_ge(rs_done, m + 1)
                nc.vector.scalar_tensor_tensor(out=nb[s][:, :, :], in0=mv[s][:, :, :, 0], scalar=-1.0,
                                               in1=rs[s][:, :, :], op0=ALU.mult, op1=ALU.mult).then_inc(nb_done, 1)

            def step(i, s):
                m = 2 * i + s
                ahead = not (isinstance(m, int) and m + 2 >= N // Q)
                moments(m, s)
                if ahead:
                    residual(m + 2, s, [scalar_part])
                finish(m, s)
                if ahead:
                    residual(m + 2, s, [vector_part])

            residual(0, 0, [scalar_part, vector_part])
            residual(1, 1, [scalar_part, vector_part])
            in_pairs(dve, step, N // Q)


def lay_out_weights(w):
    import numpy as np

    def two_blocks(m):
        both = np.zeros((2 * m.shape[0], 2 * m.shape[1]), m.dtype)
        both[:m.shape[0], :m.shape[1]] = m
        both[m.shape[0]:, m.shape[1]:] = m
        return both

    def scalar_vector(name):
        return np.concatenate([two_blocks(w[name + "0"]), two_blocks(w[name + "1"])], axis=1)

    m4 = np.concatenate([w["M4"][:, part * C:(part + 1) * C] for part in (0, 2, 3, 1)], axis=1)
    affine = np.stack([w["gamma0"], w["beta0"], w["gamma1"]], axis=1)
    parts = {
        "w_lin": scalar_vector("W_lin"), "w_self": scalar_vector("Wsc"), "w_back": scalar_vector("WB"),
        "w_m1": np.pad(two_blocks(w["M1"]), ((0, P - 2 * w["M1"].shape[0]), (0, 0))),
        "w_m2": two_blocks(w["M2"]), "w_m3": two_blocks(w["M3"]), "w_m4": two_blocks(m4),
        "poly0": np.tile(w["Wc0"], (2, 1)), "poly1": np.tile(w["Wc1"], (2, 1)), "affine": np.tile(affine, (2, 1)),
    }
    return scalar_vector("W_up"), np.concatenate([parts[name] for name, _width in WEIGHT_PARTS], axis=1)


def kernel(x, src, dst, edge_attr_16, edge_attr_4, **layer):
    import numpy as np
    import concourse.bacc as bacc
    from concourse.bass_utils import run_bass_kernel_spmd as run

    x, src, dst, rbf, sh = (np.asarray(v) for v in (x, src, dst, edge_attr_16, edge_attr_4))
    sz = Shapes(x.shape[0], src.shape[0])
    more = sz.padded_edges - sz.edges
    xp = np.pad(x, ((0, sz.rows - sz.nodes), (0, 0)))
    comps = np.concatenate([xp[:, None, :C], xp[:, C:].reshape(sz.rows, C, 3).transpose(0, 2, 1)], axis=1)
    x_cm = comps.reshape(2, sz.half, J, C).transpose(0, 3, 2, 1).reshape(P, J, sz.half)
    src_p = np.pad(src, (0, more), mode="edge").reshape(sz.groups, TG, P)
    dst_p = np.pad(dst, (0, more), mode="edge").reshape(sz.groups, TG, P)
    sh_p = np.pad(sh, ((0, more), (0, 0))).reshape(sz.groups, TG, P, 4)
    rbf_p = np.pad(rbf, ((0, more), (0, 0))).reshape(sz.groups, 2, 4 * P, 16)
    arrays = {
        "x_cm": x_cm,
        "src_idx": src_p.transpose(0, 2, 1).reshape(sz.groups * P, TG),
        "dst_pt": dst_p.transpose(2, 0, 1).reshape(P, sz.tiles),
        "dst_rows": dst_p.reshape(sz.groups, GE),
        "first_dst": dst_p[:, 0, 0].reshape(1, sz.groups),
        "sh_in": sh_p.transpose(0, 2, 1, 3).reshape(sz.groups * P, TG * 4),
        "rbf_in": rbf_p.transpose(0, 1, 3, 2).reshape(sz.groups * 32, 4 * P),
    }
    arrays["w_up"], arrays["table"] = lay_out_weights(
        {name.removeprefix("L0_gnn_"): np.asarray(v) for name, v in layer.items()})
    arrays = {name: np.ascontiguousarray(a) for name, a in arrays.items()}
    nc = bacc.Bacc("TRN2", target_bir_lowering=False, num_devices=1)
    aps = {name: nc.dram_tensor(name + "_dram", a.shape, mybir.dt.from_np(a.dtype), kind="ExternalInput").ap()
           for name, a in arrays.items()}
    out = nc.dram_tensor("out_dram", (sz.rows, F), F32, kind="ExternalOutput").ap()
    build(nc, aps["x_cm"], aps["src_idx"], aps["dst_pt"], aps["dst_rows"], aps["first_dst"], aps["sh_in"],
          aps["rbf_in"], aps["w_up"], aps["table"], out, sz)
    result = run(nc, [{name + "_dram": a for name, a in arrays.items()}], core_ids=[0])
    return result.results[0]["out_dram"][:sz.nodes]
```
